# Optimizing a Trainium2 kernel written in Bass

```python
import numpy as np
import jax
import jax.numpy as jnp

def _softmax(x, axis=-1):
    return jax.nn.softmax(x, axis=axis)

def _gelu(x):
    return jax.nn.gelu(x, approximate=True)

def _silu(x):
    return jax.nn.silu(x)

def _sigmoid(x):
    return jax.nn.sigmoid(x)

def _layernorm(x, axis=-1, eps=1e-05):
    m = jnp.mean(x, axis=axis, keepdims=True)
    v = jnp.var(x, axis=axis, keepdims=True)
    return (x - m) / jnp.sqrt(v + eps)

def _scatter_add(tgt, idx, src, axis=0):
    return tgt.at[idx].add(src)

def _segment_sum(src, seg, n):
    return jax.ops.segment_sum(src, seg, n)
kernel_name = 'mk_seq_postln_d1_jaxref_r8_08e32f'

def setup_inputs(seed: int=0):
    np.random.seed(seed)
    _w = jnp.asarray

    def _L0_attn_setup():
        import jax, jax.numpy as jnp
        import numpy as np
        DIM = 128
        HEADS = 16
        SCALE = 3
        LP = 1
        HS = DIM // HEADS

        def layer_norm(x, g, b, eps=1e-06):
            m = x.mean(-1, keepdims=True)
            v = ((x - m) ** 2).mean(-1, keepdims=True)
            return (x - m) / jnp.sqrt(v + eps) * g + b

        def windows(x, reverse):
            T = x.shape[1]
            t = jnp.arange(T)[:, None]
            i = jnp.arange(SCALE)[None, :]
            idx = t + i * LP if reverse else t - i * LP
            valid = (idx >= 0) & (idx < T)
            w = jnp.take(x, jnp.clip(idx, 0, T - 1), axis=1)
            return w * valid[None, :, :, None].astype(x.dtype)

        def local_attn(q, k, v):
            B, T, S, _ = q.shape

            def split(x):
                return x.reshape(B, T, S, HEADS, HS).transpose(0, 1, 3, 2, 4)
            qh, kh, vh = (split(q), split(k), split(v))
            scores = jnp.einsum('bthqd,bthkd->bthqk', qh, kh) / np.float32(np.sqrt(HS))
            attn = jax.nn.softmax(scores, axis=-1)
            o = jnp.einsum('bthqk,bthkd->bthqd', attn, vh)
            return o.transpose(0, 1, 3, 2, 4).reshape(B, T, S, DIM)
        key = jax.random.key(seed)
        ks = jax.random.split(key, 12)
        s = 1.0 / np.sqrt(DIM)
        inp = {'input_feature': jax.random.normal(ks[0], (2, 512, DIM), jnp.float32), 'Wq': jax.random.normal(ks[1], (DIM, DIM), jnp.float32) * s, 'bq': jnp.zeros((DIM,), jnp.float32), 'Wk': jax.random.normal(ks[2], (DIM, DIM), jnp.float32) * s, 'bk': jnp.zeros((DIM,), jnp.float32), 'Wv': jax.random.normal(ks[3], (DIM, DIM), jnp.float32) * s, 'bv': jnp.zeros((DIM,), jnp.float32), 'Wfb': jax.random.normal(ks[4], (2 * DIM, DIM), jnp.float32) * s, 'bfb': jnp.zeros((DIM,), jnp.float32), 'Wo': jax.random.normal(ks[5], (DIM, DIM), jnp.float32) * s, 'bo': jnp.zeros((DIM,), jnp.float32), 'g1': jnp.ones((DIM,), jnp.float32), 'b1': jnp.zeros((DIM,), jnp.float32), 'g2': jnp.ones((DIM,), jnp.float32), 'b2': jnp.zeros((DIM,), jnp.float32)}
        return inp
    _L0_attn_in = _L0_attn_setup()

    def _L0_ffn_setup():
        import jax, jax.numpy as jnp
        import numpy as np
        DIM = 128
        HIDDEN = 128
        NUM_EXPERTS = 8
        TOP_K = 2
        key = jax.random.key(seed)
        ks = jax.random.split(key, 8)
        std = 0.02
        x = jax.random.normal(ks[0], (2, 128, DIM), dtype=jnp.float32)
        gate_w = jax.random.normal(ks[1], (NUM_EXPERTS, DIM), dtype=jnp.float32) * std
        w1 = jax.random.normal(ks[2], (NUM_EXPERTS, DIM, HIDDEN), dtype=jnp.float32) * std
        w2 = jax.random.normal(ks[3], (NUM_EXPERTS, HIDDEN, DIM), dtype=jnp.float32) * std
        w3 = jax.random.normal(ks[4], (NUM_EXPERTS, DIM, HIDDEN), dtype=jnp.float32) * std
        w1s = jax.random.normal(ks[5], (1, DIM, HIDDEN), dtype=jnp.float32) * std
        w2s = jax.random.normal(ks[6], (1, HIDDEN, DIM), dtype=jnp.float32) * std
        w3s = jax.random.normal(ks[7], (1, DIM, HIDDEN), dtype=jnp.float32) * std
        return {'x': x, 'gate_w': gate_w, 'w1': w1, 'w2': w2, 'w3': w3, 'w1s': w1s, 'w2s': w2s, 'w3s': w3s}
    _L0_ffn_in = _L0_ffn_setup()
    _d = {'L0_attn_input_feature': _L0_attn_in['input_feature'], 'L0_attn_Wq': _L0_attn_in['Wq'], 'L0_attn_bq': _L0_attn_in['bq'], 'L0_attn_Wk': _L0_attn_in['Wk'], 'L0_attn_bk': _L0_attn_in['bk'], 'L0_attn_Wv': _L0_attn_in['Wv'], 'L0_attn_bv': _L0_attn_in['bv'], 'L0_attn_Wfb': _L0_attn_in['Wfb'], 'L0_attn_bfb': _L0_attn_in['bfb'], 'L0_attn_Wo': _L0_attn_in['Wo'], 'L0_attn_bo': _L0_attn_in['bo'], 'L0_attn_g1': _L0_attn_in['g1'], 'L0_attn_b1': _L0_attn_in['b1'], 'L0_attn_g2': _L0_attn_in['g2'], 'L0_attn_b2': _L0_attn_in['b2'], 'L0_ffn_gate_w': _L0_ffn_in['gate_w'], 'L0_ffn_w1': _L0_ffn_in['w1'], 'L0_ffn_w2': _L0_ffn_in['w2'], 'L0_ffn_w3': _L0_ffn_in['w3'], 'L0_ffn_w1s': _L0_ffn_in['w1s'], 'L0_ffn_w2s': _L0_ffn_in['w2s'], 'L0_ffn_w3s': _L0_ffn_in['w3s']}
    _x0 = _d['L0_attn_input_feature']
    _d['L0_attn_input_feature'] = jax.random.normal(jax.random.fold_in(jax.random.key(seed), 1), (32, 256, 128), dtype=_x0.dtype)
    del _x0
    return _d

def reference(L0_attn_input_feature, L0_attn_Wq, L0_attn_bq, L0_attn_Wk, L0_attn_bk, L0_attn_Wv, L0_attn_bv, L0_attn_Wfb, L0_attn_bfb, L0_attn_Wo, L0_attn_bo, L0_attn_g1, L0_attn_b1, L0_attn_g2, L0_attn_b2, L0_ffn_gate_w, L0_ffn_w1, L0_ffn_w2, L0_ffn_w3, L0_ffn_w1s, L0_ffn_w2s, L0_ffn_w3s):

    def _L0_attn_ref(input_feature, Wq, bq, Wk, bk, Wv, bv, Wfb, bfb, Wo, bo, g1, b1, g2, b2):
        import jax, jax.numpy as jnp
        import numpy as np
        DIM = 128
        HEADS = 16
        SCALE = 3
        LP = 1
        HS = DIM // HEADS

        def layer_norm(x, g, b, eps=1e-06):
            m = x.mean(-1, keepdims=True)
            v = ((x - m) ** 2).mean(-1, keepdims=True)
            return (x - m) / jnp.sqrt(v + eps) * g + b

        def windows(x, reverse):
            T = x.shape[1]
            t = jnp.arange(T)[:, None]
            i = jnp.arange(SCALE)[None, :]
            idx = t + i * LP if reverse else t - i * LP
            valid = (idx >= 0) & (idx < T)
            w = jnp.take(x, jnp.clip(idx, 0, T - 1), axis=1)
            return w * valid[None, :, :, None].astype(x.dtype)

        def local_attn(q, k, v):
            B, T, S, _ = q.shape

            def split(x):
                return x.reshape(B, T, S, HEADS, HS).transpose(0, 1, 3, 2, 4)
            qh, kh, vh = (split(q), split(k), split(v))
            scores = jnp.einsum('bthqd,bthkd->bthqk', qh, kh) / np.float32(np.sqrt(HS))
            attn = jax.nn.softmax(scores, axis=-1)
            o = jnp.einsum('bthqk,bthkd->bthqd', attn, vh)
            return o.transpose(0, 1, 3, 2, 4).reshape(B, T, S, DIM)
        x = layer_norm(input_feature, g1, b1)
        q = x @ Wq + bq
        k = x @ Wk + bk
        v = x @ Wv + bv
        out_f = local_attn(windows(q, False), windows(k, False), windows(v, False))[:, :, 1, :]
        out_r = local_attn(windows(q, True), windows(k, True), windows(v, True))[:, :, 1, :]
        out = jnp.concatenate([out_f, out_r], axis=2) @ Wfb + bfb
        out = layer_norm(out + x, g2, b2)
        return jax.nn.gelu(out @ Wo + bo, approximate=False)

    def _L0_ffn_ref(x, gate_w, w1, w2, w3, w1s, w2s, w3s):
        import jax, jax.numpy as jnp
        import numpy as np
        DIM = 128
        HIDDEN = 128
        NUM_EXPERTS = 8
        TOP_K = 2
        bs, slen, dim = x.shape
        xt = x.reshape(bs * slen, dim)
        logits = xt @ gate_w.T
        scores = jax.nn.softmax(logits.astype(jnp.float32), axis=1).astype(x.dtype)
        top_scores, sel = jax.lax.top_k(scores, TOP_K)
        sel_flat = sel.reshape(-1)
        order = jnp.argsort(sel_flat, stable=True)
        top_scores_sorted = top_scores.reshape(-1)[order]
        token_idx = order // TOP_K
        eid = sel_flat[order]
        routed_in = xt[token_idx] * top_scores_sorted[:, None]
        out_routed = jnp.zeros_like(routed_in)
        for e in range(NUM_EXPERTS):
            m = (eid == e)[:, None]
            xe = jnp.where(m, routed_in, 0.0)
            h = jax.nn.silu(xe @ w1[e]) * (xe @ w3[e])
            out_routed = out_routed + jnp.where(m, h @ w2[e], 0.0)
        hs = jax.nn.silu(xt @ w1s[0]) * (xt @ w3s[0])
        out = hs @ w2s[0]
        out = out.at[token_idx].add(out_routed)
        return out.reshape(bs, slen, dim)
    x = L0_attn_input_feature
    x = _layernorm(x + _L0_attn_ref(x, L0_attn_Wq, L0_attn_bq, L0_attn_Wk, L0_attn_bk, L0_attn_Wv, L0_attn_bv, L0_attn_Wfb, L0_attn_bfb, L0_attn_Wo, L0_attn_bo, L0_attn_g1, L0_attn_b1, L0_attn_g2, L0_attn_b2), axis=-1)
    x = _layernorm(x + _L0_ffn_ref(x, L0_ffn_gate_w, L0_ffn_w1, L0_ffn_w2, L0_ffn_w3, L0_ffn_w1s, L0_ffn_w2s, L0_ffn_w3s), axis=-1)
    return x

_drawn_inputs = setup_inputs


def setup_inputs(seed=0):
    import zlib

    import numpy as np

    out = dict(_drawn_inputs(seed))
    spreads = {'L0_attn_bq': (0.0, 0.351),
     'L0_attn_bk': (0.0, 0.8),
     'L0_attn_bv': (0.0, 0.1),
     'L0_attn_bfb': (0.0, 0.1),
     'L0_attn_bo': (0.0, 0.1),
     'L0_attn_g1': (1.0, 0.2),
     'L0_attn_b1': (0.0, 0.1),
     'L0_attn_g2': (1.0, 0.2),
     'L0_attn_b2': (0.0, 0.1)}
    factors = {'L0_ffn_gate_w': 8.0,
     'L0_ffn_w1': 8.0,
     'L0_ffn_w2': 8.0,
     'L0_ffn_w3': 8.0,
     'L0_ffn_w1s': 8.0,
     'L0_ffn_w2s': 8.0,
     'L0_ffn_w3s': 8.0}
    for name, (base, spread) in spreads.items():
        noise = np.random.default_rng([zlib.crc32(name.encode()), seed]).standard_normal(out[name].shape)
        drawn = base * np.exp(spread * noise) if base else spread * noise
        out[name] = jnp.asarray(drawn.astype(out[name].dtype))
    for name, factor in factors.items():
        out[name] = (out[name] * factor).astype(out[name].dtype)
    return out
```

```python
from contextlib import ExitStack

import numpy as np

import concourse.bass as bass
from concourse import mybir

ALU = mybir.AluOpType
ACT = mybir.ActivationFunctionType
AX = mybir.AxisListType
F32 = mybir.dt.float32
BF16 = mybir.dt.bfloat16
U32 = mybir.dt.uint32
I32 = mybir.dt.int32

P = 128
D = 128
HEADS = 16
HS = D // HEADS
NB, T = 32, 256
C = NB * T // P
W = 3
G = 4
NG = C // G + 1
E = 8
TOPK = 2
RING = 4
BS = 2 * P
CAP = NB * T + BS
NULL = E * CAP
BLOCKS = TOPK * NB * T // BS + E - 1
ROW = D + 4
NOWHERE = 1 << 20
RING3 = 8
NG4 = C // G
EPS_ATTN, EPS_OUT = 1e-6, 1e-5

K_IDENT, K_TRI, K_ONES = 0, 128, 256
K_MASKL, K_MASKR = 384, 385
K_IOTA, K_EBASE, K_HALF = 386, 394, 402
K_EPS = 414
K_BEFORE = 426
K_BLOCK, K_START = 490, 490 + BLOCKS
K_ALL = 490 + 2 * BLOCKS


def constants():
    k = np.zeros((P, K_ALL), np.float32)
    k[:, K_IDENT:K_IDENT + P] = np.eye(P)
    k[:, K_TRI:K_TRI + P] = np.triu(np.ones((P, P)), 1)
    k[:, K_ONES:K_ONES + P] = 1.0
    runs = T // C
    k[:, K_MASKL] = np.arange(P) % runs != 0
    k[:, K_MASKR] = np.arange(P) % runs != runs - 1
    k[:, K_IOTA:K_IOTA + E] = np.arange(E)
    k[:, K_EBASE:K_EBASE + E] = CAP * np.arange(E)
    k[:, K_HALF:K_HALF + 3 * G] = -0.5
    k[:, K_EPS:K_EPS + 3 * G] = np.repeat([EPS_ATTN, EPS_ATTN, EPS_OUT], G)
    k[:, K_BEFORE:K_BEFORE + E * E] = np.tri(E, E, -1).reshape(-1)
    k[:, K_BLOCK:K_BLOCK + BLOCKS] = np.arange(BLOCKS)
    k[:, K_START:K_START + BLOCKS] = BS * np.arange(BLOCKS) - NULL
    return k


def wait(eng, sem, count):
    if not (isinstance(count, int) and count <= 0):
        eng.wait_ge(sem, count)


def build(nc, a, test=None):
    with ExitStack() as ctx:
        def sb(name, shape, dt=F32):
            return ctx.enter_context(nc.sbuf_tensor(name, shape, dt))

        def psum(name, shape):
            return ctx.enter_context(nc.psum_tensor(name, shape, F32))

        def sem(name):
            return ctx.enter_context(nc.semaphore(name))

        def sems(name, n):
            return [sem(f"{name}{i}") for i in range(n)]

        x_in = a["L0_attn_input_feature"].rearrange("b (r c) d -> (b r) (c d)", c=C)
        queue_dram, back_dram = a["queue_dram"], a["back_dram"]
        back_in = back_dram.rearrange("(p c k) d -> p (c k d)", p=P, k=TOPK)
        out = a["out"].rearrange("b (r c) d -> (b r) (c d)", c=C)

        kst = sb("kst", [P, K_ALL])
        ident = kst[:, K_IDENT:K_IDENT + P]
        mask_l = kst[:, K_MASKL:K_MASKL + 1]
        mask_r = kst[:, K_MASKR:K_MASKR + 1]
        iota_e = kst[:, K_IOTA:K_IOTA + E]
        ebase = kst[:, K_EBASE:K_EBASE + E]
        minus_half = kst[:, K_HALF:K_HALF + 3 * G]
        eps3 = kst[:, K_EPS:K_EPS + 3 * G]
        tri = sb("tri", [P, P], BF16)
        ones = sb("ones", [P, P], BF16)
        wqkv = sb("wqkv", [P, 3 * D])
        wfb = sb("wfb", [P, 2, D])
        wo = sb("wo", [P, D])
        gate_t = sb("gate_t", [P, E])
        lnp = sb("lnp", [P, 4])
        bias_row = sb("bias_row", [1, 5 * D])
        bias_rest = sb("bias_rest", [1, 2, 5 * D])
        bias_part = sb("bias_part", [1, 3, 5 * D], BF16)
        bias3 = sb("bias3", [3, 5 * D], BF16)
        place = sb("place", [P, C, TOPK], U32)

        xin = sb("xin", [P, RING, G, D])
        xres = sb("xres", [P, RING, G, D])
        xh = sb("xh", [P, 2, G, D])
        xT = sb("xT", [P, RING, G, P])
        kv = sb("kv", [P, 2 + RING * G, 2, D])
        prod = sb("prod", [P, G, W, D])
        sc = sb("sc", [P, G, W, HEADS])
        smax = sb("smax", [P, G, HEADS])
        dif = sb("dif", [P, G, W, HEADS])
        ex = sb("ex", [P, G, W, HEADS])
        den = sb("den", [P, G, HEADS])
        rden = sb("rden", [P, G, HEADS])
        prob = sb("prob", [P, G, W, HEADS])
        pv = sb("pv", [P, W, G, D])
        at = sb("at", [P, 2, G, P])
        yh = sb("yh", [P, 2, G, D])
        yT = sb("yT", [P, 2, G, P])
        gz = sb("gz", [P, 2, G, D])
        r3 = sb("r3", [P, 2, G, D])
        x1g = sb("x1g", [P, 2, G, D])
        x1 = sb("x1", [P, C, D])
        x1T = sb("x1T", [P, 2, G, P])
        ln_st = sb("ln_st", [P, 3, G, 6])
        ln_mv = sb("ln_mv", [P, 2, 3, G, 2])
        ln_ve = sb("ln_ve", [P, 2, 3, G])
        ln_rs = sb("ln_rs", [P, 2, 3, G])
        ln_nb = sb("ln_nb", [P, 2, 2, G])
        top8 = sb("top8", [P, G, E])
        top8i = sb("top8i", [P, G, E], U32)
        gdif = sb("gdif", [P, G, E])
        gex = sb("gex", [P, G, E])
        gsum = sb("gsum", [P, G])
        grec = sb("grec", [P, G])
        score = sb("score", [P, 2, G, TOPK])
        hot = sb("hot", [P, G, TOPK, E])
        chosen = sb("chosen", [P, G, E], BF16)
        csum = sb("csum", [P, E])
        carry = sb("carry", [P, 2, E], BF16)
        qpos = sb("qpos", [P, G, E])
        hpos = sb("hpos", [P, G, TOPK, E])
        slot = sb("slot", [P, 2, G, TOPK], U32)
        rows = sb("rows", [P, 2, G, TOPK, ROW])

        ps_kv = psum("ps_kv", [P, G, 2, D])
        ps_q = psum("ps_q", [P, G, D])
        ps_y = psum("ps_y", [P, G, D])
        ps_z = psum("ps_z", [P, G, D])
        ps_t0 = psum("ps_t0", [P, G, P])
        ps_t1 = psum("ps_t1", [P, G, P])
        ps_s_bank = psum("ps_s", [P, G, D])
        ps_s = ps_s_bank[:, 0, 0:2 * G * E].rearrange("p (k g e) -> p k g e", k=2, g=G)

        s_w = sem("s_w")
        s_const = sem("s_const")
        s_bpart, s_bmove, s_init = sem("s_bpart"), sem("s_bmove"), sem("s_init")
        s_xin = sems("s_xin", RING)
        s_edge = sem("s_edge")
        s_xres = sems("s_xres", RING)
        s_bn, s_agg, s_ve, s_rs, s_nb = (sem("s_" + n) for n in ("bn", "agg", "ve", "rs", "nb"))
        s_xh, s_xt, s_xT = sem("s_xh"), sem("s_xt"), sem("s_xT")
        s_kvmm, s_qmm, s_kv = sem("s_kvmm"), sem("s_qmm"), sem("s_kv")
        s_prod, s_sc, s_max, s_dif, s_exp = (sem("s_" + n) for n in ("prod", "sc", "max", "dif", "exp"))
        s_msk = sem("s_msk")
        s_den, s_rden, s_prob, s_pv, s_pv0 = (sem("s_" + n) for n in ("den", "rden", "prob", "pv", "pv0"))
        s_atmm, s_at = sem("s_atmm"), sem("s_at")
        s_y, s_yh, s_yt, s_yT = sem("s_y"), sem("s_yh"), sem("s_yt"), sem("s_yT")
        s_z, s_gz, s_r3 = sem("s_z"), sem("s_gz"), sem("s_r3")
        s_x1, s_x1t, s_x1T, s_x1st = sem("s_x1"), sem("s_x1t"), sem("s_x1T"), sems("s_x1st", 2)
        s_logit, s_top, s_topi, s_gdif, s_gex = (sem("s_" + n) for n in ("logit", "top", "topi", "gdif", "gex"))
        s_gsum, s_grec, s_score, s_hot, s_chosen = (sem("s_" + n) for n in ("gsum", "grec", "score", "hot", "chosen"))
        s_csum, s_carry, s_pos, s_qpos, s_hpos, s_slot = (
            sem("s_" + n) for n in ("csum", "carry", "pos", "qpos", "hpos", "slot"))
        s_rows0, s_rows1 = sem("s_rows0"), sem("s_rows1")
        s_queue = sems("s_queue", 2)

        wall = sb("wall", [P, 3, E, D])
        wsh = sb("wsh", [P, 3, D])
        wst = sb("wst", [P, RING, 3, D])
        xs = sb("xs", [P, RING3, 2, ROW])
        xc = sb("xc", [P, RING3, D])
        xsT = sb("xsT", [P, 2, 3, P])
        silu = sb("silu", [P, 2, 3, P])
        hid = sb("hid", [P, RING, 3, P])
        ys = sb("ys", [P, RING, 2, D])
        pad = sb("pad", [P, 2, ROW])
        n_e = sb("n_e", [1, E])
        pad_at = sb("pad_at", [1, E], I32)
        nblk_u = sb("nblk_u", [1, 2, E], U32)
        nblk = sb("nblk", [1, E])
        before = sb("before", [1, E, E])
        start = sb("start", [1, E])
        end = sb("end", [1, E])
        offs = sb("offs", [1, E])
        n_be = BLOCKS * E
        flat = prod[0:1].rearrange("p g w d -> p (g w d)")
        b_ge = flat[:, 0:n_be].rearrange("p (b e) -> p b e", e=E)
        b_lt = flat[:, n_be:2 * n_be].rearrange("p (b e) -> p b e", e=E)
        flat = gz[0:1].rearrange("p s g d -> p (s g d)")
        b_in = flat[:, 0:n_be].rearrange("p (b e) -> p b e", e=E)
        flat = pv[0:1].rearrange("p w g d -> p (w g d)")
        b_v = flat[:, 0:2 * n_be].rearrange("p (k b e) -> p k b e", k=2, e=E)
        b_sum = sb("b_sum", [1, 2, BLOCKS])
        b_expert = sb("b_expert", [1, BLOCKS], I32)
        b_row = sb("b_row", [1, BLOCKS], I32)
        ps_x = (ps_t0, ps_t1)
        ps_h1 = (ps_kv[:, 0:2], ps_kv[:, 2:4])
        ps_h3 = (ps_q, ps_y)
        ps_o = (ps_z, ps_s_bank)

        yb = kv[:, 2:].rearrange("p (r g) k d -> p r g k d", r=RING)
        ysum = r3
        on = xin
        l_st = sb("l_st", [P, G, 6])
        l_mv = sb("l_mv", [P, RING, G, 2])
        l_ve = sb("l_ve", [P, RING, G])
        l_rs = sb("l_rs", [P, RING, G])
        l_nb = sb("l_nb", [P, RING, G])

        s_wx = sem("s_wx")
        s_count, s_tab = sem("s_count"), sem("s_tab")
        s_padding, s_padded = sem("s_padding"), sem("s_padded")
        s_xs = sems("s_xs", RING3)
        s_xc = sems("s_xc", RING3)
        s_wst, s_xst, s_xsT = sem("s_wst"), sem("s_xst"), sem("s_xsT")
        s_hmm, s_silu, s_hid, s_omm, s_ys, s_sh = (sem("s_" + n) for n in ("hmm", "silu", "hid", "omm", "ys", "sh"))
        s_back = sems("s_back", RING3)
        s_yb = sems("s_yb", RING)
        s_ysum, s_o, s_lst, s_lmv, s_lve, s_lrs, s_lnb, s_on = (
            sem("s_" + n) for n in ("ysum", "o", "lst", "lmv", "lve", "lrs", "lnb", "on"))
        s_out = sems("s_out", RING)

        block = ctx.enter_context(nc.Block())

        W_LOADS = 16 * (1 + 3 + 5 + 4 + 3)

        def steps(eng, body, ring, lo, hi, last):
            for t in range(lo):
                body(t, t % ring)
            with eng.Fori(lo // ring, hi // ring) as m:
                for r in range(ring):
                    body(m * ring + r, r)
            for t in range(hi, last):
                body(t, t % ring)

        def pipeline(eng, body, last):
            steps(eng, body, RING, 2 * RING, (NG - 1) // RING * RING, last)

        def over_blocks(eng, body, last):
            steps(eng, body, RING3, RING3, C, last)

        def over_output(eng, body, last):
            steps(eng, body, RING, RING, NG4, last)

        def has(b, count=BLOCKS):
            return not isinstance(b, int) or 0 <= b < count

        def upto(b, count=BLOCKS):
            return min(b, count - 1) + 1 if isinstance(b, int) else b + 1

        def ring_count(b, rb, ring, each):
            return (b - rb) * (each // ring) + each if not isinstance(b, int) or b >= 0 else 0

        def runs(g, first=0):
            return not isinstance(g, int) or first <= g < NG

        def done(g, first=0):
            return min(g, NG - 1) + 1 - first if isinstance(g, int) else g + (1 - first)

        TABLE = 18
        HUB = NG - 1 + 5 + 1

        def hub(t):
            return min(t, HUB - 1) + 1 if isinstance(t, int) else t + 1

        def res_count(g, rg):
            return (g - rg) * (16 // RING) + (16 if rg >= 1 else 0)

        def store_count(g, odd, each=16):
            return g * (each // 2) + (each // 2) * odd

        def tokens(c):
            return x1[:, c] if isinstance(c, int) else x1[:, bass.ds(c, 1)].rearrange("p o d -> p (o d)")

        def in_count(g, rg):
            return (g - rg) * (16 // RING) + 16

        def apart(eng, count):
            if not isinstance(count, int):
                eng.to_reg(count)
                eng.wait_ge(s_init, 1)

        @block.sync
        def _(sp):
            def load_in(g, r):
                if isinstance(g, int) and g == 0:
                    sp.dma_start(xin[:, 0, 2:4], x_in[:, 0:2 * D]).then_inc(s_xin[0], 16)
                    sp.dma_start(xin[1:P, 0, 0:2], x_in[0:P - 1, (C - 2) * D:C * D]).then_inc(s_edge, 16)
                    sp.dma_start(xin[0:1, 0, 0:2], x_in[0:1, 0:2 * D]).then_inc(s_edge, 16)
                elif isinstance(g, int) and g == NG - 1:
                    sp.dma_start(xin[:, r, 0:2], x_in[:, (C - 2) * D:C * D]).then_inc(s_xin[r], 16)
                    sp.dma_start(xin[0:P - 1, r, 2:4], x_in[1:P, 0:2 * D]).then_inc(s_edge, 16)
                    sp.dma_start(xin[P - 1:P, r, 2:4], x_in[0:1, 0:2 * D]).then_inc(s_edge, 16)
                else:
                    sp.dma_start(xin[:, r], x_in[:, bass.ds(g * (G * D) - 2 * D, G * D)]).then_inc(s_xin[r], 16)

            for g in range(RING):
                load_in(g, g)

            def load(dst, src):
                sp.dma_start(dst, src).then_inc(s_w, 16)

            load(kst[:], a["shape_consts"])
            for i, n in enumerate(("Wq", "Wk", "Wv")):
                load(wqkv[:, i * D:(i + 1) * D], a["L0_attn_" + n])
            for i, n in enumerate(("bq", "bk", "bv", "bfb", "bo")):
                load(bias_row[:, i * D:(i + 1) * D], a["L0_attn_" + n].rearrange("(o d) -> o d", o=1))
            for i, n in enumerate(("g1", "b1", "g2", "b2")):
                load(lnp[:, i:i + 1], a["L0_attn_" + n].rearrange("(d o) -> d o", o=1))
            load(wfb[:], a["L0_attn_Wfb"].rearrange("(h k) n -> k h n", h=2))
            load(wo[:], a["L0_attn_Wo"])
            with nc.allow_non_contiguous_dma(reason="1024 gate weights, once"):
                load(gate_t[:], a["L0_ffn_gate_w"].rearrange("e d -> d e"))

            for i, n in enumerate("132"):
                sp.dma_start(wall[:, i], a["L0_ffn_w" + n].rearrange("e k n -> k e n")).then_inc(s_wx, 16)
                sp.dma_start(wsh[:, i:i + 1], a["L0_ffn_w" + n + "s"].rearrange("e k n -> k e n")).then_inc(s_wx, 16)

            def body(t, r):
                g = t
                if runs(g) and not (isinstance(g, int) and g < RING):
                    wait(sp, s_xh, done(g - RING))
                    load_in(g, r)
                g, rg = t - 4, (r - 4) % RING
                if runs(g, 1):
                    wait(sp, s_r3, done(g - RING, 1))
                    sp.dma_start(xres[:, rg], x_in[:, bass.ds(g * (G * D) - G * D, G * D)]).then_inc(s_xres[rg], 16)

                g, rg = t - 7, (r - 7) % RING
                if runs(g, 1):
                    wait(sp, s_x1, done(g, 1))
                    sp.dma_start(x1[:, bass.ds(g * G - G, G)], x1g[:, rg % 2]).then_inc(s_x1st[rg % 2], 16)

            pipeline(sp, body, NG + 7)

            sp.wait_ge(s_padding, 2)
            pad_rows = queue_dram[NULL:NULL + BS, :].rearrange("(p u) w -> p u w", u=2)
            sp.dma_start(pad_rows, pad[:]).then_inc(s_padded, 16)
            sp.wait_ge(s_tab, 2)
            for e in range(E):
                at = sp.value_load(pad_at[0:1, e:e + 1], min_val=e * CAP, max_val=e * CAP + NB * T)
                sp.dma_start(queue_dram[bass.ds(at, BS), :].rearrange("(p u) w -> p u w", u=2), pad[:]).then_inc(s_padded, 16)
            sp.wait_ge(s_padded, 16 * (E + 1))
            for i in range(2):
                sp.wait_ge(s_queue[i], store_count(NG - 1 - (NG - 1 - i) % 2, i, 16 * TOPK * G))
            sp.wait_ge(s_tab, TABLE)

            for i in range(2):
                sp.wait_ge(s_x1st[i], store_count(NG - 1 - (NG - 1 - i) % 2, i))

            def fetch(b, rb):
                if not has(b):
                    return
                if has(b, C):
                    wait(sp, s_sh, upto(b - RING3))
                    sp.dma_start(xc[:, rb], tokens(b)).then_inc(s_xc[rb], 16)
                wait(sp, s_back[rb], ring_count(b - RING3, rb, RING3, 32))
                row = sp.value_load(b_row[0:1, bass.ds(b, 1)], min_val=0, max_val=NULL)
                sp.dma_start(xs[:, rb], queue_dram[bass.ds(row, BS), :].rearrange("(p u) w -> p u w", u=2)).then_inc(s_xs[rb], 16)

            over_blocks(sp, fetch, BLOCKS)

            for rb in range(RING3):
                sp.wait_ge(s_back[rb], 32 * ((BLOCKS - 1 - rb) // RING3 + 1))

            def body(t, r):
                if has(t, NG4):
                    wait(sp, s_ysum, upto(t - RING, NG4))
                    sp.dma_start(yb[:, r], back_in[:, bass.ds(t * (G * TOPK * D), G * TOPK * D)]).then_inc(s_yb[r], 16)
                g, rg = t - 3, (r - 3) % RING
                if has(g, NG4):
                    sp.wait_ge(s_on, upto(g, NG4))
                    sp.dma_start(out[:, bass.ds(g * (G * D), G * D)], on[:, rg]).then_inc(s_out[rg], 16)

            over_output(sp, body, NG4 + 3)
            for r in range(RING):
                sp.wait_ge(s_out[r], 16 * (NG4 // RING))

        @block.gpsimd
        def _(pool):
            pool.iota(place[:], pattern=[[TOPK, C], [1, TOPK]], base=0, channel_multiplier=TOPK * C).then_inc(s_init, 1)
            pool.memset(at[:, 1], 0.0).then_inc(s_init, 1)
            pool.memset(kv[:, 0:2], 0.0).then_inc(s_init, 1)
            pool.memset(xT[:, RING - 1], 0.0).then_inc(s_init, 1)
            pool.memset(ln_mv[:], 1.0).then_inc(s_init, 1)
            pool.memset(carry[:, 0], 0.0).then_inc(s_init, 1)
            pool.memset(rows[:, :, :, :, D:ROW], 0.0).then_inc(s_init, 1)
            pool.memset(pad[:, :, 0:D], 0.0).then_inc(s_padding, 1)
            pool.memset(pad[:, :, D:ROW].bitcast(I32), NOWHERE).then_inc(s_padding, 1)
            pool.wait_ge(s_bpart, 3)
            for i in range(3):
                pool.dma_start(bias3[i:i + 1, :], bias_part[:, i, :]).then_inc(s_bmove, 16)

            def scatter(g, rg, i0, i1):
                if not runs(g, 1):
                    return
                apart(pool, done(g, 1))
                pool.wait_ge(s_slot, done(g, 1))
                pool.wait_ge(s_rows0, done(g, 1))
                pool.wait_ge(s_rows1, done(g, 1))
                for i in range(i0, i1):
                    for k in range(TOPK):
                        pool.indirect_dma_start(queue_dram, bass.IndirectOffsetOnAxis(ap=slot[:, rg % 2, i, k:k + 1], axis=0),
                                                rows[:, rg % 2, i, k], None).then_inc(s_queue[rg % 2], 16)

            def body(t, r):
                scatter(t - 7, (r - 7) % RING, 0, 2)
                if not isinstance(t, int) or t < HUB:
                    pool.wait_ge(s_ve, hub(t))
                    wait(pool, s_xh, done(t - 2))
                    wait(pool, s_yh, done(t - 5, 1))
                    wait(pool, s_x1, done(t - 7, 1))
                    pool.tensor_tensor(ln_rs[:, r % 2].rearrange("p k g -> p (k g)"),
                                       ln_ve[:, r % 2].rearrange("p k g -> p (k g)"), minus_half, ALU.pow).then_inc(s_rs, 1)
                g = t - 2
                if runs(g):
                    rg = (r - 2) % RING
                    pool.wait_ge(s_prob, done(g))
                    wait(pool, s_atmm, done(g - 1))
                    for j in range(2):
                        ins = pool.tensor_tensor(
                            pv[:, j].rearrange("p g (h d) -> p g h d", h=HEADS),
                            kv[:, G * rg + j:G * rg + j + G, 1].rearrange("p g (h d) -> p g h d", h=HEADS),
                            prob[:, :, j].unsqueeze(3).to_broadcast([P, G, HEADS, HS]), ALU.mult)
                    ins.then_inc(s_pv0, 1)
                g = t - 4
                if runs(g, 1):
                    rg = (r - 4) % RING
                    pool.wait_ge(s_gz, done(g, 1))
                    pool.wait_ge(s_xres[rg], res_count(g, rg))
                    wait(pool, s_x1, done(g - 2, 1))
                    pool.tensor_tensor(r3[:, rg % 2], gz[:, rg % 2], xres[:, rg], ALU.add).then_inc(s_r3, 1)
                scatter(t - 7, (r - 7) % RING, 2, 4)

            pipeline(pool, body, NG + 7)

            def give_back(t, r):
                b, rb = t - 3, (r - 3) % RING3
                if has(b):
                    apart(pool, upto(b))
                    pool.wait_ge(s_ys, upto(b))
                    for u in range(2):
                        pool.indirect_dma_start(back_dram, bass.IndirectOffsetOnAxis(ap=xs[:, rb, u, D:D + 1].bitcast(U32), axis=0),
                                                ys[:, rb % RING, u], None, bounds_check=NB * T * TOPK - 1,
                                                oob_is_err=False).then_inc(s_back[rb], 16)

            over_blocks(pool, give_back, BLOCKS + 3)

            def body(t, r):
                if has(t, NG4):
                    pool.wait_ge(s_yb[r], ring_count(t, r, RING, 16))
                    wait(pool, s_o, upto(t - 2, NG4))
                    pool.tensor_tensor(ysum[:, r % 2], yb[:, r, :, 0], yb[:, r, :, 1], ALU.add).then_inc(s_ysum, 1)
                g, rg = t - 1, (r - 1) % RING
                if has(g, NG4):
                    pool.wait_ge(s_lve, upto(g, NG4))
                    wait(pool, s_lnb, upto(g - RING, NG4))
                    pool.tensor_tensor(l_rs[:, rg], l_ve[:, rg], minus_half[:, 0:G], ALU.pow).then_inc(s_lrs, 1)

            over_output(pool, body, NG4 + 1)

        @block.vector
        def _(dve):
            dve.wait_ge(s_w, W_LOADS)
            dve.tensor_copy(tri[:], kst[:, K_TRI:K_TRI + P]).then_inc(s_const, 1)
            dve.tensor_copy(ones[:], kst[:, K_ONES:K_ONES + P]).then_inc(s_const, 1)
            dve.tensor_copy(bias_part[:, 0], bias_row[:]).then_inc(s_bpart, 1)
            dve.wait_ge(s_bpart, 1)
            dve.tensor_tensor(bias_rest[:, 0], bias_row[:], bias_part[:, 0], ALU.subtract).then_inc(s_const, 1)
            dve.wait_ge(s_const, 3)
            dve.tensor_copy(bias_part[:, 1], bias_rest[:, 0]).then_inc(s_bpart, 1)
            dve.wait_ge(s_bpart, 2)
            dve.tensor_tensor(bias_rest[:, 1], bias_rest[:, 0], bias_part[:, 1], ALU.subtract).then_inc(s_const, 1)
            dve.wait_ge(s_const, 4)
            dve.tensor_copy(bias_part[:, 2], bias_rest[:, 1]).then_inc(s_bpart, 1)
            dve.wait_ge(s_init, 7)

            def scores(g, rg):
                dve.wait_ge(s_qmm, done(g))
                dve.wait_ge(s_kv, done(g))
                k0 = kv[:, G * rg:G * rg + G, 0]
                window = bass.AP(k0.tensor, k0.offset, [list(k0.ap[0]), [2 * D, G], [2 * D, W], [1, D]])
                dve.tensor_tensor(prod[:], ps_q[:].unsqueeze(2).to_broadcast([P, G, W, D]), window,
                                  ALU.mult).then_inc(s_prod, 1)
                dve.wait_ge(s_prod, done(g))
                dve.tensor_reduce(sc[:], prod[:].rearrange("p g w (h d) -> p (g w h) d", h=HEADS),
                                  AX.X, ALU.add).then_inc(s_sc, 1)
                dve.wait_ge(s_sc, done(g))
                if isinstance(g, int) and g in (0, NG - 1):
                    i, m = (2, mask_l) if g == 0 else (3, mask_r)
                    dve.tensor_scalar(sc[:, i], sc[:, i], m, None, ALU.mult).then_inc(s_msk, 1)
                    dve.wait_ge(s_msk, 1 if g == 0 else 2)
                dve.tensor_reduce(smax[:], sc[:].rearrange("p g w h -> p g h w"), AX.X, ALU.max).then_inc(s_max, 1)
                dve.wait_ge(s_max, done(g))
                dve.tensor_tensor(dif[:], sc[:], smax[:].unsqueeze(2).to_broadcast([P, G, W, HEADS]),
                                  ALU.subtract).then_inc(s_dif, 1)

            def norms(t, r):
                r2 = r % 2
                parts = []
                apart(dve, hub(t))
                if runs(t - 3, 1):
                    dve.wait_ge(s_y, done(t - 3, 1))
                    parts.append((1, ps_y))
                if runs(t - 5, 1):
                    dve.wait_ge(s_r3, done(t - 5, 1))
                    parts.append((2, r3[:, (r - 5) % 2]))
                if runs(t):
                    dve.wait_ge(s_xin[r], in_count(t, r))
                    if isinstance(t, int) and t in (0, NG - 1):
                        dve.wait_ge(s_edge, 32 if t == 0 else 64)
                    parts.append((0, xin[:, r]))
                for kind, src in parts:
                    for i in range(G):
                        ins = dve.bn_stats(ln_st[:, kind, i], src[:, i])
                ins.then_inc(s_bn, 1)
                apart(dve, hub(t))
                dve.wait_ge(s_bn, hub(t))
                for kind, src in parts:
                    for i in range(G):
                        ins = dve.bn_aggr(ln_mv[:, r2, kind, i], ln_st[:, kind, i])
                ins.then_inc(s_agg, 1)
                dve.wait_ge(s_agg, hub(t))
                wait(dve, s_rs, hub(t - 2) if not isinstance(t, int) or t >= 2 else 0)
                dve.tensor_tensor(ln_ve[:, r2], ln_mv[:, r2, :, :, 1], eps3.rearrange("p (k g) -> p k g", k=3),
                                  ALU.add).then_inc(s_ve, 1)

            def weigh(g, rg):
                dve.wait_ge(s_exp, done(g))
                dve.tensor_reduce(den[:], ex[:].rearrange("p g w h -> p g h w"), AX.X, ALU.add).then_inc(s_den, 1)
                dve.wait_ge(s_den, done(g))
                dve.reciprocal(rden[:], den[:]).then_inc(s_rden, 1)
                dve.wait_ge(s_rden, done(g))
                wait(dve, s_pv0, done(g - 1))
                dve.tensor_tensor(prob[:], ex[:], rden[:].unsqueeze(2).to_broadcast([P, G, W, HEADS]),
                                  ALU.mult).then_inc(s_prob, 1)
                dve.wait_ge(s_prob, done(g))
                wait(dve, s_atmm, done(g - 1))
                dve.tensor_tensor(pv[:, 2].rearrange("p g (h d) -> p g h d", h=HEADS),
                                  kv[:, G * rg + 2:G * rg + 2 + G, 1].rearrange("p g (h d) -> p g h d", h=HEADS),
                                  prob[:, :, 2].unsqueeze(3).to_broadcast([P, G, HEADS, HS]), ALU.mult).then_inc(s_pv, 1)

            def choose(g):
                apart(dve, done(g, 1))
                dve.wait_ge(s_logit, done(g, 1))
                for i in range(G):
                    ins = dve.max(top8[:, i], ps_s[:, 0, i])
                ins.then_inc(s_top, 1)
                apart(dve, done(g, 1))
                dve.wait_ge(s_top, done(g, 1))
                for i in range(G):
                    ins = dve.max_index(top8i[:, i], top8[:, i], ps_s[:, 0, i])
                ins.then_inc(s_topi, 1)
                wait(dve, s_gex, done(g - 1, 1))
                dve.tensor_tensor(gdif[:], top8[:], top8[:, :, 0:1].to_broadcast([P, G, E]), ALU.subtract).then_inc(s_gdif, 1)
                dve.wait_ge(s_topi, done(g, 1))
                dve.tensor_tensor(hot[:], iota_e.unsqueeze(1).unsqueeze(1).to_broadcast([P, G, TOPK, E]),
                                  top8i[:, :, 0:TOPK].unsqueeze(3).to_broadcast([P, G, TOPK, E]),
                                  ALU.is_equal).then_inc(s_hot, 1)
                dve.wait_ge(s_hot, done(g, 1))
                wait(dve, s_pos, done(g - 1, 1))
                dve.tensor_tensor(chosen[:], hot[:, :, 0], hot[:, :, 1], ALU.add).then_inc(s_chosen, 1)

            def enqueue(g, rg):
                g2 = rg % 2
                dve.wait_ge(s_chosen, done(g, 1))
                dve.tensor_reduce(csum[:], chosen[:].rearrange("p g e -> p e g"), AX.X, ALU.add).then_inc(s_csum, 1)
                dve.wait_ge(s_gex, done(g, 1))
                dve.tensor_reduce(gsum[:], gex[:], AX.X, ALU.add).then_inc(s_gsum, 1)
                dve.wait_ge(s_csum, done(g, 1))
                dve.tensor_tensor(carry[:, g2], carry[:, 1 - g2], csum[:], ALU.add).then_inc(s_carry, 1)
                dve.wait_ge(s_gsum, done(g, 1))
                dve.reciprocal(grec[:], gsum[:]).then_inc(s_grec, 1)
                dve.wait_ge(s_pos, done(g, 1))
                dve.tensor_tensor(qpos[:], ps_s[:, 1], ebase.unsqueeze(1).to_broadcast([P, G, E]), ALU.add).then_inc(s_qpos, 1)
                dve.wait_ge(s_grec, done(g, 1))
                wait(dve, s_rows1, done(g - 2, 1))
                dve.tensor_tensor(score[:, g2], gex[:, :, 0:TOPK], grec[:].unsqueeze(2).to_broadcast([P, G, TOPK]),
                                  ALU.mult).then_inc(s_score, 1)
                dve.wait_ge(s_qpos, done(g, 1))
                dve.tensor_tensor(hpos[:], hot[:], qpos[:].unsqueeze(2).to_broadcast([P, G, TOPK, E]), ALU.mult).then_inc(s_hpos, 1)
                wait(dve, s_queue[g2], store_count(g - 2, g2, 16 * TOPK * G))
                dve.tensor_copy(rows[:, g2, :, :, D:D + 1].bitcast(U32), place[:, bass.ds(g * G - G, G)].unsqueeze(3))
                dve.wait_ge(s_score, done(g, 1))
                dve.tensor_tensor(rows[:, g2, :, 0, 0:D], x1g[:, g2], score[:, g2, :, 0:1].to_broadcast([P, G, D]),
                                  ALU.mult).then_inc(s_rows0, 1)
                dve.wait_ge(s_hpos, done(g, 1))
                with nc.allow_low_precision(reason="a whole number below 2 ** 24 among zeros"):
                    dve.tensor_reduce(slot[:, g2], hpos[:], AX.X, ALU.add).then_inc(s_slot, 1)

            def body(t, r):
                if runs(t - 2):
                    scores(t - 2, (r - 2) % RING)
                if runs(t - 6, 1):
                    choose(t - 6)
                if not isinstance(t, int) or t < HUB:
                    norms(t, r)
                if runs(t - 2):
                    weigh(t - 2, (r - 2) % RING)
                if runs(t - 6, 1):
                    enqueue(t - 6, (r - 6) % RING)
                if not isinstance(t, int) or t < HUB:
                    dve.wait_ge(s_rs, hub(t))
                    wait(dve, s_xh, done(t - 2))
                    wait(dve, s_yh, done(t - 5, 1))
                    dve.scalar_tensor_tensor(ln_nb[:, r % 2], ln_mv[:, r % 2, 0:2, :, 0], -1.0, ln_rs[:, r % 2, 0:2],
                                             ALU.mult, ALU.mult).then_inc(s_nb, 1)
                g, rg = t - 5, (r - 5) % RING
                if runs(g, 1):
                    wait(dve, s_x1t, done(g - 2, 1))
                    wait(dve, s_rows1, done(g - 2, 1))
                    wait(dve, s_x1st[rg % 2], store_count(g - 2, rg % 2))
                    for i in range(G):
                        ins = dve.tensor_scalar(x1g[:, rg % 2, i], r3[:, rg % 2, i], ln_mv[:, r % 2, 2, i, 0:1],
                                                ln_rs[:, r % 2, 2, i:i + 1], ALU.subtract, ALU.mult)
                    ins.then_inc(s_x1, 1)

            pipeline(dve, body, NG + 6)

            dve.wait_ge(s_count, 1)
            dve.tensor_copy(n_e[:], ps_s_bank[0:1, 0, 0:E]).then_inc(s_tab, 1)
            tab = [1]

            def table(instruction, *args, **kw):
                dve.wait_ge(s_tab, tab[0])
                instruction(*args, **kw).then_inc(s_tab, 1)
                tab[0] += 1

            def row(first, n):
                return kst[0:1, first:first + n]

            def each_e(ap):
                return ap.unsqueeze(1).to_broadcast([1, BLOCKS, E])

            def each_b(ap):
                return ap.unsqueeze(2).to_broadcast([1, BLOCKS, E])

            with nc.allow_low_precision(reason="whole numbers below 2 ** 24"):
                table(dve.tensor_tensor, pad_at[:], n_e[:], row(K_EBASE, E), ALU.add)
                table(dve.tensor_scalar, nblk_u[:, 0], n_e[:], float(BS - 1), None, ALU.add)
                table(dve.tensor_scalar, nblk_u[:, 1], nblk_u[:, 0], BS.bit_length() - 1, None, ALU.logical_shift_right)
                table(dve.tensor_copy, nblk[:], nblk_u[:, 1])
                table(dve.tensor_tensor, before[:], row(K_BEFORE, E * E).rearrange("o (e j) -> o e j", e=E),
                      nblk[:].unsqueeze(1).to_broadcast([1, E, E]), ALU.mult)
                table(dve.tensor_reduce, start[:], before[:], AX.X, ALU.add)
                table(dve.tensor_tensor, end[:], start[:], nblk[:], ALU.add)
                table(dve.scalar_tensor_tensor, offs[:], start[:], -float(BS), row(K_EBASE, E), ALU.mult, ALU.add)
                table(dve.tensor_tensor, b_ge[:], each_b(row(K_BLOCK, BLOCKS)), each_e(start[:]), ALU.is_ge)
                table(dve.tensor_tensor, b_lt[:], each_b(row(K_BLOCK, BLOCKS)), each_e(end[:]), ALU.is_lt)
                table(dve.tensor_tensor, b_in[:], b_ge[:], b_lt[:], ALU.mult)
                table(dve.tensor_tensor, b_v[:, 1], b_in[:], each_e(row(K_IOTA, E)), ALU.mult)
                table(dve.tensor_tensor, b_v[:, 0], each_b(row(K_START, BLOCKS)), each_e(offs[:]), ALU.add)
                table(dve.tensor_tensor, b_v[:, 0], b_v[:, 0], b_in[:], ALU.mult)
                table(dve.tensor_reduce, b_sum[:], b_v[:], AX.X, ALU.add)
                table(dve.tensor_copy, b_expert[:], b_sum[:, 1])
                table(dve.tensor_scalar, b_row[:], b_sum[:, 0], float(NULL), None, ALU.add)
            assert tab[0] == TABLE

            def body(t, r):
                q = r % 2
                b, rb = t - 3, (r - 3) % RING3
                if has(b, C):
                    dve.wait_ge(s_ys, upto(b))
                    col = tokens(b)
                    dve.tensor_tensor(col, col, ps_o[rb % 2][:, 2], ALU.add).then_inc(s_sh, 1)
                b = t
                if has(b):
                    dve.wait_ge(s_xst, upto(b))
                    wait(dve, s_hmm, upto(b - 2))
                    n = 3 if has(b, C) else 2
                    dve.tensor_copy(xsT[:, q, 0:n], ps_x[q][:, 0:n]).then_inc(s_xsT, 1)
                b, rb = t - 1, (r - 1) % RING3
                if has(b):
                    dve.wait_ge(s_silu, upto(b))
                    wait(dve, s_omm, upto(b - RING))
                    n = 3 if has(b, C) else 2
                    dve.tensor_tensor(hid[:, rb % RING, 0:n], silu[:, rb % 2, 0:n], ps_h3[rb % 2][:, 0:n], ALU.mult).then_inc(s_hid, 1)

            over_blocks(dve, body, BLOCKS + 3)
            dve.wait_ge(s_sh, C)

            def body(t, r):
                g, rg = t - 1, (r - 1) % RING
                if has(g, NG4):
                    dve.wait_ge(s_lrs, upto(g, NG4))
                    wait(dve, s_on, upto(g - RING, NG4))
                    dve.scalar_tensor_tensor(l_nb[:, rg], l_mv[:, rg, :, 0], -1.0, l_rs[:, rg], ALU.mult, ALU.mult).then_inc(s_lnb, 1)
                if has(t, NG4):
                    at = t * G
                    o = x1[:, bass.ds(at, G)]
                    dve.wait_ge(s_ysum, upto(t, NG4))
                    dve.tensor_tensor(o, o, ysum[:, r % 2], ALU.add).then_inc(s_o, 1)
                    apart(dve, upto(t, NG4))
                    dve.wait_ge(s_o, upto(t, NG4))
                    for i in range(G):
                        ins = dve.bn_stats(l_st[:, i], tokens(at + i))
                    ins.then_inc(s_lst, 1)
                    apart(dve, upto(t, NG4))
                    dve.wait_ge(s_lst, upto(t, NG4))
                    for i in range(G):
                        ins = dve.bn_aggr(l_mv[:, r, i], l_st[:, i])
                    ins.then_inc(s_lmv, 1)
                    dve.wait_ge(s_lmv, upto(t, NG4))
                    dve.tensor_tensor(l_ve[:, r], l_mv[:, r, :, 1], eps3[:, 2 * G:3 * G], ALU.add).then_inc(s_lve, 1)

            over_output(dve, body, NG4 + 1)

        @block.scalar
        def _(act):
            act.wait_ge(s_w, W_LOADS)
            act.wait_ge(s_init, 7)

            def body(t, r):
                l2 = (r - 1) % 2
                g, rg = t - 4, (r - 4) % RING
                if runs(g, 1):
                    act.wait_ge(s_nb, hub(t - 1))
                    wait(act, s_yt, done(g - 2, 1))
                    for i in range(G):
                        ins = act.activation(yh[:, rg % 2, i], ps_y[:, i], ACT.Identity,
                                             bias=ln_nb[:, l2, 1, i:i + 1], scale=ln_rs[:, l2, 1, i:i + 1])
                    ins.then_inc(s_yh, 1)
                g, rg = t - 1, (r - 1) % RING
                if runs(g):
                    act.wait_ge(s_nb, hub(t - 1))
                    wait(act, s_xt, done(g - 2))
                    for i in range(G):
                        ins = act.activation(xh[:, rg % 2, i], xin[:, rg, i], ACT.Identity,
                                             bias=ln_nb[:, l2, 0, i:i + 1], scale=ln_rs[:, l2, 0, i:i + 1])
                    ins.then_inc(s_xh, 1)
                    act.wait_ge(s_xt, done(g))
                    wait(act, s_y, done(g - 3, 1))
                    act.activation(xT[:, rg], ps_t0[:], ACT.Identity, bias=lnp[:, 1:2], scale=lnp[:, 0:1]).then_inc(s_xT, 1)
                g, rg = t - 4, (r - 4) % RING
                if runs(g, 1):
                    act.wait_ge(s_yt, done(g, 1))
                    wait(act, s_z, done(g - 2, 1))
                    act.activation(yT[:, rg % 2], ps_t1[:], ACT.Identity, bias=lnp[:, 3:4], scale=lnp[:, 2:3]).then_inc(s_yT, 1)
                g, rg = t - 2, (r - 2) % RING
                if runs(g):
                    act.wait_ge(s_dif, done(g))
                    act.activation(ex[:], dif[:], ACT.Exp, scale=float(1.0 / np.sqrt(HS))).then_inc(s_exp, 1)
                g = t - 6
                if runs(g, 1):
                    act.wait_ge(s_gdif, done(g, 1))
                    wait(act, s_score, done(g - 1, 1))
                    act.activation(gex[:], gdif[:], ACT.Exp).then_inc(s_gex, 1)
                g, rg = t - 1, (r - 1) % RING
                if runs(g):
                    act.wait_ge(s_kvmm, done(g))
                    wait(act, s_pv, done(g - 3))
                    wait(act, s_pv0, done(g - 3))
                    at0 = 2 + G * rg
                    if isinstance(g, int) and g == 0:
                        act.activation(kv[:, at0:at0 + 2], ps_kv[:, 0:2], ACT.Identity, scale=mask_l)
                        act.activation(kv[:, at0 + 2:at0 + 4], ps_kv[:, 2:4], ACT.Identity).then_inc(s_kv, 1)
                    elif isinstance(g, int) and g == NG - 1:
                        act.activation(kv[:, at0:at0 + 2], ps_kv[:, 0:2], ACT.Identity)
                        act.activation(kv[:, at0 + 2:at0 + 4], ps_kv[:, 2:4], ACT.Identity, scale=mask_r).then_inc(s_kv, 1)
                    else:
                        ins = act.activation(kv[:, at0:at0 + G], ps_kv[:], ACT.Identity)
                        if rg == RING - 1:
                            ins = act.activation(kv[:, 0:2], ps_kv[:, 2:4], ACT.Identity)
                        ins.then_inc(s_kv, 1)
                g, rg = t - 4, (r - 4) % RING
                if runs(g, 1):
                    act.wait_ge(s_z, done(g, 1))
                    wait(act, s_r3, done(g - 2, 1))
                    act.activation(gz[:, rg % 2], ps_z[:], ACT.Gelu).then_inc(s_gz, 1)
                g, rg = t - 2, (r - 2) % RING
                if runs(g):
                    act.wait_ge(s_atmm, done(g))
                    wait(act, s_y, done(g - 1, 1))
                    act.activation(at[:, rg % 2], ps_t1[:], ACT.Identity).then_inc(s_at, 1)
                g, rg = t - 6, (r - 6) % RING
                if runs(g, 1):
                    act.wait_ge(s_score, done(g, 1))
                    wait(act, s_queue[rg % 2], store_count(g - 2, rg % 2, 16 * TOPK * G))
                    for i in range(G):
                        ins = act.activation(rows[:, rg % 2, i, 1, 0:D], x1g[:, rg % 2, i], ACT.Identity,
                                             scale=score[:, rg % 2, i, 1:2])
                    ins.then_inc(s_rows1, 1)
                g, rg = t - 5, (r - 5) % RING
                if runs(g, 1):
                    act.wait_ge(s_x1t, done(g, 1))
                    wait(act, s_logit, done(g - 2, 1))
                    act.activation(x1T[:, rg % 2], ps_t0[:], ACT.Identity).then_inc(s_x1T, 1)

            pipeline(act, body, NG + 6)
            act.wait_ge(s_wx, 96)
            act.wait_ge(s_tab, TABLE)

            def body(t, r):
                b, rb = t, r
                if has(b):
                    wait(act, s_omm, upto(b - RING))
                    e = act.value_load(b_expert[0:1, bass.ds(b, 1)], min_val=0, max_val=E - 1)
                    act.activation(wst[:, rb % RING], wall[:, :, bass.ds(e, 1)].rearrange("p w o d -> p w (o d)"),
                                   ACT.Identity).then_inc(s_wst, 1)
                b, rb = t - 3, (r - 3) % RING3
                if has(b):
                    act.wait_ge(s_omm, upto(b))
                    wait(act, s_back[(rb - RING) % RING3], ring_count(b - RING, (rb - RING) % RING3, RING3, 32))
                    act.activation(ys[:, rb % RING], ps_o[rb % 2][:, 0:2], ACT.Identity).then_inc(s_ys, 1)
                b, rb = t - 1, (r - 1) % RING3
                if has(b):
                    act.wait_ge(s_hmm, upto(b))
                    wait(act, s_hid, upto(b - 2))
                    n = 3 if has(b, C) else 2
                    act.activation(silu[:, rb % 2, 0:n], ps_h1[rb % 2].rearrange("p g k d -> p (g k) d")[:, 0:n],
                                   ACT.Silu).then_inc(s_silu, 1)

            over_blocks(act, body, BLOCKS + 3)

            def body(t, r):
                g, rg = t - 1, (r - 1) % RING
                if has(g, NG4):
                    act.wait_ge(s_lnb, upto(g, NG4))
                    wait(act, s_out[rg], ring_count(g - RING, rg, RING, 16))
                    for i in range(G):
                        ins = act.activation(on[:, rg, i], tokens(g * G + i), ACT.Identity,
                                             bias=l_nb[:, rg, i:i + 1], scale=l_rs[:, rg, i:i + 1])
                    ins.then_inc(s_on, 1)

            over_output(act, body, NG4 + 1)

        @block.tensor
        def _(pe):
            ones3 = ones[0:3, :]

            def bias(out, part, width, copies):
                row = bias3[:, part * D:part * D + width].unsqueeze(1).to_broadcast([3, copies, width])
                pe.matmul(out, ones3, row, start=True, stop=False, skip_group_check=True)

            def add(out, lhsT, rhs, stop):
                return pe.matmul(out, lhsT, rhs, start=False, stop=stop, skip_group_check=True)

            pe.wait_ge(s_w, W_LOADS)
            pe.wait_ge(s_const, 4)
            pe.wait_ge(s_bmove, 48)
            pe.wait_ge(s_init, 7)

            def body(t, r):
                g, rg = t - 6, (r - 6) % RING
                if runs(g, 1):
                    pe.wait_ge(s_x1T, done(g, 1))
                    wait(pe, s_qpos, done(g - 1, 1))
                    for i in range(G):
                        mm = pe.matmul(ps_s[:, 0, i], x1T[:, rg % 2, i], gate_t[:], start=True, stop=True, skip_group_check=True)
                    mm.then_inc(s_logit, 1)
                g, rg = t - 3, (r - 3) % RING
                if runs(g, 1):
                    pe.wait_ge(s_at, done(g))
                    wait(pe, s_yh, done(g - 1, 1))
                    rp = (rg - 1) % RING
                    bias(ps_y[:], 3, D, G)
                    for i in range(G):
                        add(ps_y[:, i], xT[:, rp, i + 2] if i < 2 else xT[:, rg, i - 2], ident, False)
                        add(ps_y[:, i], at[:, rp % 2, i + 2] if i < 2 else at[:, rg % 2, i - 2], wfb[:, 0], False)
                        mm = add(ps_y[:, i], at[:, rg % 2, i], wfb[:, 1], True)
                    mm.then_inc(s_y, 1)
                g, rg = t - 1, (r - 1) % RING
                if runs(g):
                    pe.wait_ge(s_xh, done(g))
                    wait(pe, s_x1T, done(g - 5, 1))
                    for i in range(G):
                        mm = pe.transpose(ps_t0[:, i], xh[:, rg % 2, i], ident)
                    mm.then_inc(s_xt, 1)
                g, rg = t - 4, (r - 4) % RING
                if runs(g, 1):
                    pe.wait_ge(s_yh, done(g, 1))
                    wait(pe, s_at, done(t - 3))
                    for i in range(G):
                        mm = pe.transpose(ps_t1[:, i], yh[:, rg % 2, i], ident)
                    mm.then_inc(s_yt, 1)
                g, rg = t - 1, (r - 1) % RING
                if runs(g):
                    pe.wait_ge(s_xT, done(g))
                    wait(pe, s_kv, done(g - 1))
                    for h in range(2):
                        bias(ps_kv[:, 2 * h:2 * h + 2].rearrange("p g k d -> p g (k d)"), 1, 2 * D, 2)
                        for i in range(2 * h, 2 * h + 2):
                            mm = add(ps_kv[:, i].rearrange("p k d -> p (k d)"), xT[:, rg, i], wqkv[:, D:3 * D], True)
                    mm.then_inc(s_kvmm, 1)
                    wait(pe, s_prod, done(g - 1))
                    bias(ps_q[:], 0, D, G)
                    for i in range(G):
                        mm = add(ps_q[:, i], xT[:, (rg - 1) % RING, G - 1] if i == 0 else xT[:, rg, i - 1], wqkv[:, 0:D], True)
                    mm.then_inc(s_qmm, 1)
                g, rg = t - 6, (r - 6) % RING
                if runs(g, 1):
                    pe.wait_ge(s_chosen, done(g, 1))
                    wait(pe, s_carry, done(g - 1, 1))
                    pe.matmul(ps_s[:, 1], tri[:], chosen[:], start=True, stop=False, skip_group_check=True)
                    for i in range(G - 1):
                        add(ps_s[:, 1, i + 1:G], ones[:], chosen[:, i:i + 1].to_broadcast([P, G - 1 - i, E]), False)
                    add(ps_s[:, 1], ones[:], carry[:, 1 - rg % 2].unsqueeze(1).to_broadcast([P, G, E]), True).then_inc(s_pos, 1)
                g, rg = t - 4, (r - 4) % RING
                if runs(g, 1):
                    pe.wait_ge(s_yT, done(g, 1))
                    wait(pe, s_gz, done(g - 1, 1))
                    bias(ps_z[:], 4, D, G)
                    for i in range(G):
                        mm = add(ps_z[:, i], yT[:, rg % 2, i], wo[:], True)
                    mm.then_inc(s_z, 1)
                g, rg = t - 2, (r - 2) % RING
                if runs(g):
                    pe.wait_ge(s_pv, done(g))
                    pe.wait_ge(s_pv0, done(g))
                    wait(pe, s_at, done(g - 1))
                    for i in range(G):
                        for j in range(W):
                            mm = pe.matmul(ps_t1[:, i], pv[:, j, i], ident, start=(j == 0), stop=(j == W - 1))
                    mm.then_inc(s_atmm, 1)
                g, rg = t - 5, (r - 5) % RING
                if runs(g, 1):
                    pe.wait_ge(s_x1, done(g, 1))
                    wait(pe, s_x1T, done(g - 1, 1))
                    for i in range(G):
                        mm = pe.transpose(ps_t0[:, i], x1g[:, rg % 2, i], ident)
                    mm.then_inc(s_x1t, 1)

            pipeline(pe, body, NG + 6)

            pe.wait_ge(s_carry, NG - 1)
            pe.wait_ge(s_hpos, NG - 1)
            pe.matmul(ps_s_bank[:, 0, 0:E], ones[:], carry[:, (NG - 1) % 2], start=True, stop=True).then_inc(s_count, 1)
            pe.wait_ge(s_wx, 96)
            pe.wait_ge(s_tab, 1)

            def body(t, r):
                b, rb = t, r
                if has(b):
                    pe.wait_ge(s_xs[rb], ring_count(b, rb, RING3, 16))
                    wait(pe, s_xsT, upto(b - 2))
                    for u in range(2):
                        mm = pe.transpose(ps_x[rb % 2][:, u], xs[:, rb, u, 0:D], ident)
                    if has(b, C):
                        pe.wait_ge(s_xc[rb], ring_count(b, rb, RING3, 16))
                        mm = pe.transpose(ps_x[rb % 2][:, 2], xc[:, rb], ident)
                    mm.then_inc(s_xst, 1)
                b, rb = t - 1, (r - 1) % RING3
                if has(b):
                    q = rb % 2
                    pe.wait_ge(s_xsT, upto(b))
                    pe.wait_ge(s_wst, upto(b))
                    wait(pe, s_hid, upto(b - 2))
                    h1 = ps_h1[q].rearrange("p g k d -> p (g k) d")
                    for w, ps in ((0, h1), (1, ps_h3[q])):
                        mm = pe.matmul(ps[:, 0:2], wst[:, rb % RING, w], xsT[:, q, 0:2], start=True, stop=True)
                        if has(b, C):
                            mm = pe.matmul(ps[:, 2], wsh[:, w], xsT[:, q, 2], start=True, stop=True)
                    mm.then_inc(s_hmm, 1)
                b, rb = t - 3, (r - 3) % RING3
                if has(b):
                    pe.wait_ge(s_hid, upto(b))
                    wait(pe, s_ys, upto(b - 2))
                    wait(pe, s_sh, upto(b - 2, C))
                    for u in range(2):
                        mm = pe.matmul(ps_o[rb % 2][:, u], hid[:, rb % RING, u], wst[:, rb % RING, 2], start=True, stop=True)
                    if has(b, C):
                        mm = pe.matmul(ps_o[rb % 2][:, 2], hid[:, rb % RING, 2], wsh[:, 2], start=True, stop=True)
                    mm.then_inc(s_omm, 1)

            over_blocks(pe, body, BLOCKS + 3)


_INS = ["L0_attn_input_feature"] + ["L0_attn_" + n for n in (
    "Wq", "bq", "Wk", "bk", "Wv", "bv", "Wfb", "bfb", "Wo", "bo", "g1", "b1", "g2", "b2")] + [
    "L0_ffn_" + n for n in ("gate_w", "w1", "w2", "w3", "w1s", "w2s", "w3s")]


def kernel(**inputs):
    import concourse.bacc as _bacc
    from concourse.bass_utils import run_bass_kernel_spmd as _run

    nc = _bacc.Bacc("TRN2", target_bir_lowering=False, num_devices=1)
    arrays, a = {}, {}
    for name, value in [(n, inputs[n]) for n in _INS] + [("shape_consts", constants())]:
        value = np.ascontiguousarray(value)
        arrays[f"in_{name}"] = value
        a[name] = nc.dram_tensor(f"in_{name}", value.shape, mybir.dt.from_np(value.dtype), kind="ExternalInput").ap()
    a["queue_dram"] = nc.dram_tensor("queue_dram", (NULL + BS, ROW), F32).ap()
    a["back_dram"] = nc.dram_tensor("back_dram", (NB * T * TOPK, D), F32).ap()
    a["out"] = nc.dram_tensor("out_0", (NB, T, D), F32, kind="ExternalOutput").ap()
    build(nc, a)
    return _run(nc, [arrays], core_ids=[0]).results[0]["out_0"]
```

```python
from contextlib import ExitStack

import numpy as np

import concourse.bass as bass
from concourse import mybir

ALU = mybir.AluOpType
ACT = mybir.ActivationFunctionType
AX = mybir.AxisListType
F32 = mybir.dt.float32
BF16 = mybir.dt.bfloat16
U32 = mybir.dt.uint32
I32 = mybir.dt.int32

P = 128
D = 128
HEADS = 16
HS = D // HEADS
NB, T = 32, 256
C = NB * T // P
W = 3
G = 4
NG = C // G + 1
E = 8
TOPK = 2
RING = 4
BS = 2 * P
CAP = NB * T + BS
NULL = E * CAP
BLOCKS = TOPK * NB * T // BS + E - 1
ROW = D + 4
SCORE, FIRST, WHERE = D, D + 2, D + 3
NOWHERE = 1 << 20
RING3 = 8
NG4 = C // G
EPS_ATTN, EPS_OUT = 1e-6, 1e-5
EXP_LN = "natural_log_exp_and_others"

K_IDENT, K_TRI, K_ONES = 0, 128, 256
K_MASKL, K_MASKR = 384, 385
K_IOTA, K_EBASE, K_HALF = 386, 394, 402
K_EPS = 414
K_BEFORE = 426
K_BLOCK, K_START = 490, 490 + BLOCKS
K_PART = 490 + 2 * BLOCKS
K_ALL = K_PART + 3
W_QKV, W_FB, W_O, W_GATE, W_LN, W_ALL = 0, 3 * D, 5 * D, 6 * D, 6 * D + E, 6 * D + E + 4


def constants():
    k = np.zeros((P, K_ALL), np.float32)
    k[:, K_IDENT:K_IDENT + P] = np.eye(P)
    k[:, K_TRI:K_TRI + P] = np.triu(np.ones((P, P)), 1)
    k[:, K_ONES:K_ONES + P] = 1.0
    runs = T // C
    k[:, K_MASKL] = np.arange(P) % runs != 0
    k[:, K_MASKR] = np.arange(P) % runs != runs - 1
    k[:, K_IOTA:K_IOTA + E] = np.arange(E)
    k[:, K_EBASE:K_EBASE + E] = CAP * np.arange(E)
    k[:, K_HALF:K_HALF + 3 * G] = -0.5
    k[:, K_EPS:K_EPS + 3 * G] = np.repeat([EPS_ATTN, EPS_ATTN, EPS_OUT], G)
    k[:, K_BEFORE:K_BEFORE + E * E] = np.tri(E, E, -1).reshape(-1)
    k[:, K_BLOCK:K_BLOCK + BLOCKS] = np.arange(BLOCKS)
    k[:, K_START:K_START + BLOCKS] = BS * np.arange(BLOCKS) - NULL
    k[:3, K_PART:K_PART + 3] = np.eye(3)
    return k


def pack(inputs):
    att = {n: np.asarray(inputs["L0_attn_" + n]) for n in
           ("Wq", "Wk", "Wv", "Wfb", "Wo", "g1", "b1", "g2", "b2", "bq", "bk", "bv", "bfb", "bo")}
    ffn = {n: np.asarray(inputs["L0_ffn_" + n]) for n in ("gate_w", "w1", "w3", "w2", "w1s", "w3s", "w2s")}
    columns = [constants(), att["Wq"], att["Wk"], att["Wv"], att["Wfb"][:D], att["Wfb"][D:], att["Wo"],
               ffn["gate_w"].T, *(att[n][:, None] for n in ("g1", "b1", "g2", "b2"))]
    biases = np.concatenate([att[n] for n in ("bq", "bk", "bv", "bfb", "bo")])[None]
    experts = np.stack([np.concatenate([ffn[n], ffn[n + "s"]]).transpose(1, 0, 2) for n in ("w1", "w3", "w2")], 1)
    return {"packed": np.concatenate(columns, 1), "biases": biases, "experts": experts}


def wait(eng, sem, count):
    if not (isinstance(count, int) and count <= 0):
        eng.wait_ge(sem, count)


def build(nc, a, test=None):
    with ExitStack() as ctx:
        def sb(name, shape, dt=F32):
            return ctx.enter_context(nc.sbuf_tensor(name, shape, dt))

        def psum(name, shape):
            return ctx.enter_context(nc.psum_tensor(name, shape, F32))

        def sem(name):
            return ctx.enter_context(nc.semaphore(name))

        def sems(name, n):
            return [sem(f"{name}{i}") for i in range(n)]

        x_in = a["L0_attn_input_feature"].rearrange("b (r c) d -> (b r) (c d)", c=C)
        queue_dram, back_dram = a["queue_dram"], a["back_dram"]
        back_in = back_dram.rearrange("(p c k) d -> p (c k d)", p=P, k=TOPK)
        out = a["out"].rearrange("b (r c) d -> (b r) (c d)", c=C)

        packed = sb("packed", [P, K_ALL + W_ALL])
        kst = packed[:, 0:K_ALL]
        weights = packed[:, K_ALL:]
        ident = kst[:, K_IDENT:K_IDENT + P]
        mask_l = kst[:, K_MASKL:K_MASKL + 1]
        mask_r = kst[:, K_MASKR:K_MASKR + 1]
        iota_e = kst[:, K_IOTA:K_IOTA + E]
        ebase = kst[:, K_EBASE:K_EBASE + E]
        minus_half = kst[:, K_HALF:K_HALF + 3 * G]
        eps3 = kst[:, K_EPS:K_EPS + 3 * G]
        tri = sb("tri", [P, P], BF16)
        ones = sb("ones", [P, P], BF16)
        wqkv = weights[:, W_QKV:W_QKV + 3 * D]
        wfb = weights[:, W_FB:W_FB + 2 * D].rearrange("p (h d) -> p h d", h=2)
        wo = weights[:, W_O:W_O + D]
        gate_t = weights[:, W_GATE:W_GATE + E]
        lnp = weights[:, W_LN:W_LN + 4]
        bias_row = sb("bias_row", [3, 5 * D])
        bias_rest = sb("bias_rest", [3, 2, 5 * D])
        bias_part = sb("bias_part", [3, 3, 5 * D], BF16)
        bias_some = sb("bias_some", [3, 2, 5 * D])
        bias3 = sb("bias3", [3, 5 * D], BF16)
        place = sb("place", [P, C])
        place_i = sb("place_i", [P, C], I32)

        x_both = sb("x_both", [P, 2 * RING * G * D])
        xin = x_both[:, 0:RING * G * D].rearrange("p (r g d) -> p r g d", r=RING, g=G)
        xres = x_both[:, RING * G * D:].rearrange("p (r g d) -> p r g d", r=RING, g=G)
        xh = sb("xh", [P, 2, G, D])
        xT = sb("xT", [P, RING, G, P])
        kv = sb("kv", [P, 2 + RING * G, 2, D])
        prod = sb("prod", [P, G, W, D])
        sc = sb("sc", [P, G, W, HEADS])
        smax = sb("smax", [P, G, HEADS])
        dif = sb("dif", [P, G, W, HEADS])
        ex = sb("ex", [P, G, W, HEADS])
        den = sb("den", [P, G, HEADS])
        rden = sb("rden", [P, G, HEADS])
        prob = sb("prob", [P, G, W, HEADS])
        pv = sb("pv", [P, W, G, D])
        at = sb("at", [P, 2, G, P])
        yh = sb("yh", [P, 2, G, D])
        yT = sb("yT", [P, 2, G, P])
        gz = sb("gz", [P, 2, G, D])
        r3 = sb("r3", [P, 2, G, D])
        x1g = sb("x1g", [P, RING, G, ROW])
        x1 = sb("x1", [P, C, D])
        x1T = sb("x1T", [P, 2, G, P])
        ln_st = sb("ln_st", [P, 3, G, 6])
        ln_mv = sb("ln_mv", [P, 2, 3, G, 2])
        ln_ve = sb("ln_ve", [P, 2, 3, G])
        ln_log = sb("ln_log", [P, 3, G])
        ln_rs = sb("ln_rs", [P, 2, 3, G])
        ln_nb = sb("ln_nb", [P, 2, 3, G])
        top8 = sb("top8", [P, G, E])
        top8i = sb("top8i", [P, G, E], U32)
        gdif = sb("gdif", [P, G, E])
        gex = sb("gex", [P, G, E])
        gsum = sb("gsum", [P, G])
        grec = sb("grec", [P, G])
        hot = sb("hot", [P, G, TOPK, E])
        chosen = sb("chosen", [P, G, E], BF16)
        csum = sb("csum", [P, E])
        carry = sb("carry", [P, 2, E], BF16)
        qpos = sb("qpos", [P, G, E])
        hpos = sb("hpos", [P, G, TOPK, E])
        slot = sb("slot", [P, 2, G, TOPK], U32)

        ps_kv = psum("ps_kv", [P, G, 2, D])
        ps_q = psum("ps_q", [P, G, D])
        ps_y = psum("ps_y", [P, G, D])
        ps_z = psum("ps_z", [P, G, D])
        ps_t0 = psum("ps_t0", [P, G, P])
        ps_t1 = psum("ps_t1", [P, G, P])
        ps_s_bank = psum("ps_s", [P, G, D])
        ps_s = ps_s_bank[:, 0, 0:2 * G * E].rearrange("p (k g e) -> p k g e", k=2, g=G)

        s_w, s_bias = sem("s_w"), sem("s_bias")
        s_const = sem("s_const")
        s_bpart, s_init = sem("s_bpart"), sem("s_init")
        s_xin = sems("s_xin", RING)
        s_edge = sem("s_edge")
        s_xres = sems("s_xres", RING)
        s_obn, s_bn, s_agg, s_ve, s_log, s_rs, s_nb = (sem("s_" + n) for n in ("obn", "bn", "agg", "ve", "log", "rs", "nb"))
        s_xh, s_xt, s_xT = sem("s_xh"), sem("s_xt"), sem("s_xT")
        s_kvmm, s_qmm, s_kv = sem("s_kvmm"), sem("s_qmm"), sem("s_kv")
        s_prod, s_sc, s_max, s_dif, s_exp = (sem("s_" + n) for n in ("prod", "sc", "max", "dif", "exp"))
        s_msk = sem("s_msk")
        s_den, s_rden, s_prob, s_pv, s_pv0 = (sem("s_" + n) for n in ("den", "rden", "prob", "pv", "pv0"))
        s_atmm, s_at = sem("s_atmm"), sem("s_at")
        s_y, s_yh, s_yt, s_yT = sem("s_y"), sem("s_yh"), sem("s_yt"), sem("s_yT")
        s_z, s_gz, s_r3 = sem("s_z"), sem("s_gz"), sem("s_r3")
        s_x1, s_x1t, s_x1T, s_x1st = sem("s_x1"), sem("s_x1t"), sem("s_x1T"), sems("s_x1st", RING)
        s_logit, s_top, s_topi, s_gdif, s_gex = (sem("s_" + n) for n in ("logit", "top", "topi", "gdif", "gex"))
        s_gsum, s_grec, s_score, s_hot, s_chosen = (sem("s_" + n) for n in ("gsum", "grec", "score", "hot", "chosen"))
        s_csum, s_carry, s_pos, s_qpos, s_hpos, s_slot = (
            sem("s_" + n) for n in ("csum", "carry", "pos", "qpos", "hpos", "slot"))
        s_meta = sem("s_meta")
        s_queue = sems("s_queue", RING)

        wall = sb("wall", [P, 3, E + 1, D])
        wsh = wall[:, :, E]
        wst = sb("wst", [P, RING, 3, D])
        xs = sb("xs", [P, RING3, 2, ROW])
        xc = sb("xc", [P, RING3, D])
        xsc = sb("xsc", [P, 2, 2, D])
        part = sb("part", [P, RING, 2, 2])
        xscore = sb("xscore", [P, RING, 2])
        where = sb("where", [P, RING3, 2], U32)
        xsT = sb("xsT", [P, 2, 3, P])
        silu = sb("silu", [P, 2, 3, P])
        hid = sb("hid", [P, RING, 3, P])
        ys = sb("ys", [P, RING, 2, D])
        pad = sb("pad", [P, 2, ROW])
        n_e = sb("n_e", [P, E])
        pad_at = sb("pad_at", [P, E], I32)
        nblk_u = sb("nblk_u", [P, 2, E], U32)
        nblk = sb("nblk", [P, E])
        before = sb("before", [P, E, E])
        start = sb("start", [P, E])
        end = sb("end", [P, E])
        offs = sb("offs", [P, E])
        n_be = BLOCKS * E
        flat = prod[:].rearrange("p g w d -> p (g w d)")
        b_ge = flat[:, 0:n_be].rearrange("p (b e) -> p b e", e=E)
        b_lt = flat[:, n_be:2 * n_be].rearrange("p (b e) -> p b e", e=E)
        flat = gz[:].rearrange("p s g d -> p (s g d)")
        b_in = flat[:, 0:n_be].rearrange("p (b e) -> p b e", e=E)
        flat = pv[:].rearrange("p w g d -> p (w g d)")
        b_v = flat[:, 0:2 * n_be].rearrange("p (k b e) -> p k b e", k=2, e=E)
        b_sum = sb("b_sum", [P, 2, BLOCKS])
        b_expert = sb("b_expert", [P, BLOCKS], I32)
        b_row = sb("b_row", [P, BLOCKS], I32)
        ps_x = (ps_t0, ps_t1)
        ps_h1 = [ps_kv[:, 2 * q:2 * q + 2].rearrange("p g k d -> p (g k) d") for q in range(2)]
        ps_h3 = (ps_q, ps_y)
        ps_o = (ps_z, ps_s_bank)

        yb = x_both[:].rearrange("p (r g k d) -> p r g k d", r=RING, g=G, k=TOPK)
        ysum = r3
        on = kv[:, 2:2 + RING * G // 2].rearrange("p (r h) k d -> p r (h k) d", r=RING)
        l_st = sb("l_st", [P, G, 6])
        l_mv = sb("l_mv", [P, RING, G, 2])
        l_ve = sb("l_ve", [P, RING, G])
        l_rs = sb("l_rs", [P, RING, G])
        l_nb = sb("l_nb", [P, RING, G])

        s_wx = sem("s_wx")
        s_count, s_tab = sem("s_count"), sem("s_tab")
        s_padding, s_padded = sem("s_padding"), sem("s_padded")
        s_xs = sems("s_xs", RING3)
        s_xc = sems("s_xc", RING3)
        s_part, s_xscore, s_xsc, s_where = (sem("s_" + n) for n in ("part", "xscore", "xsc", "where"))
        s_wst, s_xst, s_xsT = sem("s_wst"), sem("s_xst"), sem("s_xsT")
        s_hmm, s_silu, s_hid, s_omm, s_ys, s_sh = (sem("s_" + n) for n in ("hmm", "silu", "hid", "omm", "ys", "sh"))
        s_back = sems("s_back", RING3)
        s_yb = sems("s_yb", RING)
        s_ysum, s_o, s_lst, s_lmv, s_lve, s_lrs, s_lnb, s_on = (
            sem("s_" + n) for n in ("ysum", "o", "lst", "lmv", "lve", "lrs", "lnb", "on"))
        s_out = sems("s_out", RING)

        block = ctx.enter_context(nc.Block())


        def steps(eng, body, ring, lo, hi, last):
            for t in range(lo):
                body(t, t % ring)
            with eng.Fori(lo // ring, hi // ring) as m:
                for r in range(lo % ring, lo % ring + ring):
                    body(m * ring + r, r % ring)
            for t in range(hi, last):
                body(t, t % ring)

        def pipeline(eng, body, last, lo=2 * RING + 1):
            steps(eng, body, RING, lo, NG - 1 + lo % RING, last)

        def over_blocks(eng, body, last):
            steps(eng, body, RING3, RING3, C, last)

        def over_output(eng, body, last):
            steps(eng, body, RING, 2 * RING, NG4, last)

        def has(b, count=BLOCKS):
            return not isinstance(b, int) or 0 <= b < count

        def upto(b, count=BLOCKS):
            return min(b, count - 1) + 1 if isinstance(b, int) else b + 1

        def ring_count(b, rb, ring, each):
            return (b - rb) * (each // ring) + each if not isinstance(b, int) or b >= 0 else 0

        def runs(g, first=0):
            return not isinstance(g, int) or first <= g < NG

        def done(g, first=0):
            return min(g, NG - 1) + 1 - first if isinstance(g, int) else g + (1 - first)

        TABLE = 18
        HUB = NG - 1 + 6 + 1

        def hub(t):
            return min(t, HUB - 1) + 1 if isinstance(t, int) else t + 1

        def slot_count(g, rg, each=16):
            return (g - rg) * (each // RING) + (each if rg >= 1 else 0) if not isinstance(g, int) or g >= 1 else 0

        def tokens(c):
            return x1[:, c] if isinstance(c, int) else x1[:, bass.ds(c, 1)].rearrange("p o d -> p (o d)")

        def in_count(g, rg):
            return (g - rg) * (16 // RING) + 16

        def apart(eng, count):
            if not isinstance(count, int):
                eng.to_reg(count)
                eng.wait_ge(s_init, 1)

        @block.sync
        def _(sp):
            def load_in(g, r):
                if isinstance(g, int) and g == 0:
                    sp.dma_start(xin[:, 0, 2:4], x_in[:, 0:2 * D]).then_inc(s_xin[0], 16)
                    sp.dma_start(xin[1:P, 0, 0:2], x_in[0:P - 1, (C - 2) * D:C * D]).then_inc(s_edge, 16)
                    sp.dma_start(xin[0:1, 0, 0:2], x_in[0:1, 0:2 * D]).then_inc(s_edge, 16)
                elif isinstance(g, int) and g == NG - 1:
                    sp.dma_start(xin[0:P - 1, r, 2:4], x_in[1:P, 0:2 * D]).then_inc(s_edge, 16)
                    sp.dma_start(xin[P - 1:P, r, 2:4], x_in[0:1, 0:2 * D]).then_inc(s_edge, 16)
                    sp.wait_ge(s_edge, 64)
                    sp.dma_start(xin[:, r, 0:2], x_in[:, (C - 2) * D:C * D]).then_inc(s_xin[r], 16)
                else:
                    sp.dma_start(xin[:, r], x_in[:, bass.ds(g * (G * D) - 2 * D, G * D)]).then_inc(s_xin[r], 16)

            sp.dma_start(bias_row[:], a["biases"].to_broadcast([3, 5 * D])).then_inc(s_bias, 16)
            sp.dma_start(packed[:], a["packed"]).then_inc(s_w, 16)
            for g in range(RING):
                load_in(g, g)
            sp.dma_start(wall[:], a["experts"]).then_inc(s_wx, 16)

            def body(t, r):
                g = t
                if runs(g) and not (isinstance(g, int) and g < RING):
                    wait(sp, s_xh, done(g - RING))
                    load_in(g, r)
                g, rg = t - 3, (r - 3) % RING
                if runs(g, 1):
                    wait(sp, s_r3, done(g - RING, 1))
                    sp.dma_start(xres[:, rg], x_in[:, bass.ds(g * (G * D) - G * D, G * D)]).then_inc(s_xres[rg], 16)

                g, rg = t - 7, (r - 7) % RING
                if runs(g, 1):
                    wait(sp, s_x1, done(g, 1))
                    sp.dma_start(x1[:, bass.ds(g * G - G, G)], x1g[:, rg, :, 0:D]).then_inc(s_x1st[rg], 16)

            pipeline(sp, body, NG + 7, 2 * RING)

            sp.wait_ge(s_padding, 2)
            pad_rows = queue_dram[NULL:NULL + BS, :].rearrange("(p u) w -> p u w", u=2)
            sp.dma_start(pad_rows, pad[:]).then_inc(s_padded, 16)
            sp.wait_ge(s_tab, 2)
            for e in range(E):
                at = sp.value_load(pad_at[0:1, e:e + 1], min_val=e * CAP, max_val=e * CAP + NB * T)
                sp.dma_start(queue_dram[bass.ds(at, BS), :].rearrange("(p u) w -> p u w", u=2), pad[:]).then_inc(s_padded, 16)
            sp.wait_ge(s_padded, 16 * (E + 1))
            for i in range(RING):
                sp.wait_ge(s_queue[i], 16 * TOPK * G * (C // G // RING))
            sp.wait_ge(s_tab, TABLE)

            for i in range(RING):
                sp.wait_ge(s_x1st[i], 16 * (C // G // RING))

            def fetch(b, rb):
                if not has(b):
                    return
                if has(b, C):
                    wait(sp, s_sh, upto(b - RING3))
                    sp.dma_start(xc[:, rb], tokens(b)).then_inc(s_xc[rb], 16)
                wait(sp, s_xsc, upto(b - RING3))
                wait(sp, s_where, upto(b - RING3))
                row = sp.value_load(b_row[0:1, bass.ds(b, 1)], min_val=0, max_val=NULL)
                sp.dma_start(xs[:, rb], queue_dram[bass.ds(row, BS), :].rearrange("(p u) w -> p u w", u=2)).then_inc(s_xs[rb], 16)

            over_blocks(sp, fetch, BLOCKS)

            for rb in range(RING3):
                sp.wait_ge(s_back[rb], 32 * ((BLOCKS - 1 - rb) // RING3 + 1))

            def body(t, r):
                if has(t, NG4):
                    wait(sp, s_ysum, upto(t - RING, NG4))
                    sp.dma_start(yb[:, r], back_in[:, bass.ds(t * (G * TOPK * D), G * TOPK * D)]).then_inc(s_yb[r], 16)
                g, rg = t - 8, (r - 8) % RING
                if has(g, NG4):
                    sp.wait_ge(s_on, upto(g, NG4))
                    sp.dma_start(out[:, bass.ds(g * (G * D), G * D)], on[:, rg]).then_inc(s_out[rg], 16)

            over_output(sp, body, NG4 + 8)
            for r in range(RING):
                sp.wait_ge(s_out[r], 16 * (NG4 // RING))

        @block.gpsimd
        def _(pool):
            pool.iota(place_i[:], pattern=[[TOPK, C]], base=0, channel_multiplier=TOPK * C).then_inc(s_init, 1)
            pool.memset(at[:, 1], 0.0).then_inc(s_init, 1)
            pool.memset(kv[:, 0:2], 0.0).then_inc(s_init, 1)
            pool.memset(x1g[:, :, :, D:ROW], 0.0).then_inc(s_init, 1)
            pool.memset(xT[:, RING - 1], 0.0).then_inc(s_init, 1)
            pool.memset(ln_mv[:], 1.0).then_inc(s_init, 1)
            pool.memset(carry[:, 0], 0.0).then_inc(s_init, 1)
            pool.memset(pad[:, :, 0:WHERE], 0.0).then_inc(s_padding, 1)
            pool.memset(pad[:, :, WHERE:ROW], float(NOWHERE)).then_inc(s_padding, 1)

            def scatter(g, rg, i0, i1):
                if not runs(g, 1):
                    return
                apart(pool, done(g, 1))
                pool.wait_ge(s_slot, done(g, 1))
                pool.wait_ge(s_meta, done(g, 1))
                for i in range(i0, i1):
                    for k in range(TOPK):
                        pool.indirect_dma_start(queue_dram, bass.IndirectOffsetOnAxis(ap=slot[:, rg % 2, i, k:k + 1], axis=0),
                                                x1g[:, rg, i], None).then_inc(s_queue[rg], 16)

            def body(t, r):
                g = t - 3
                if runs(g):
                    rg = (r - 3) % RING
                    pool.wait_ge(s_prob, done(g))
                    wait(pool, s_atmm, done(g - 1))
                    for j in range(2):
                        ins = pool.tensor_tensor(
                            pv[:, j].rearrange("p g (h d) -> p g h d", h=HEADS),
                            kv[:, G * rg + j:G * rg + j + G, 1].rearrange("p g (h d) -> p g h d", h=HEADS),
                            prob[:, :, j].unsqueeze(3).to_broadcast([P, G, HEADS, HS]), ALU.mult)
                    ins.then_inc(s_pv0, 1)
                scatter(t - 8, (r - 8) % RING, 0, 2)
                g = t - 5
                if runs(g, 1):
                    rg = (r - 5) % RING
                    pool.wait_ge(s_gz, done(g, 1))
                    pool.wait_ge(s_xres[rg], slot_count(g, rg))
                    wait(pool, s_x1, done(g - 2, 1))
                    pool.tensor_tensor(r3[:, rg % 2], gz[:, rg % 2], xres[:, rg], ALU.add).then_inc(s_r3, 1)
                scatter(t - 8, (r - 8) % RING, 2, 4)

            pipeline(pool, body, NG + 8)

            def give_back(t, r):
                b, rb = t - 2, (r - 2) % RING3
                if has(b):
                    apart(pool, upto(b))
                    pool.wait_ge(s_ys, upto(b))
                    pool.wait_ge(s_where, upto(b))
                    for u in range(2):
                        pool.indirect_dma_start(back_dram, bass.IndirectOffsetOnAxis(ap=where[:, rb, u:u + 1], axis=0),
                                                ys[:, rb % RING, u], None, bounds_check=NB * T * TOPK - 1,
                                                oob_is_err=False).then_inc(s_back[rb], 16)

            over_blocks(pool, give_back, BLOCKS + 2)

            def body(t, r):
                if has(t, NG4):
                    pool.wait_ge(s_yb[r], ring_count(t, r, RING, 16))
                    wait(pool, s_o, upto(t - 2, NG4))
                    pool.tensor_tensor(ysum[:, r % 2], yb[:, r, :, 0], yb[:, r, :, 1], ALU.add).then_inc(s_ysum, 1)
                g, rg = t - 3, (r - 3) % RING
                if has(g, NG4):
                    pool.wait_ge(s_lve, upto(g, NG4))
                    wait(pool, s_on, upto(g - RING, NG4))
                    pool.tensor_tensor(l_rs[:, rg], l_ve[:, rg], minus_half[:, 0:G], ALU.pow).then_inc(s_lrs, 1)

            over_output(pool, body, NG4 + 3)

        @block.vector
        def _(dve):
            dve.wait_ge(s_bias, 16)
            dve.tensor_copy(bias_part[:, 0], bias_row[:]).then_inc(s_bpart, 1)
            dve.wait_ge(s_bpart, 1)
            dve.tensor_tensor(bias_rest[:, 0], bias_row[:], bias_part[:, 0], ALU.subtract).then_inc(s_bpart, 1)
            dve.wait_ge(s_bpart, 2)
            dve.tensor_copy(bias_part[:, 1], bias_rest[:, 0]).then_inc(s_bpart, 1)
            dve.wait_ge(s_bpart, 3)
            dve.tensor_tensor(bias_rest[:, 1], bias_rest[:, 0], bias_part[:, 1], ALU.subtract).then_inc(s_bpart, 1)
            dve.wait_ge(s_bpart, 4)
            dve.tensor_copy(bias_part[:, 2], bias_rest[:, 1]).then_inc(s_bpart, 1)
            dve.wait_ge(s_w, 16)
            dve.wait_ge(s_bpart, 5)
            dve.tensor_scalar(bias_some[:, 0], bias_part[:, 0], kst[0:3, K_PART:K_PART + 1], None, ALU.mult).then_inc(s_bpart, 1)
            dve.wait_ge(s_bpart, 6)
            dve.scalar_tensor_tensor(bias_some[:, 1], bias_part[:, 1], kst[0:3, K_PART + 1:K_PART + 2], bias_some[:, 0],
                                     ALU.mult, ALU.add).then_inc(s_bpart, 1)
            dve.wait_ge(s_bpart, 7)
            dve.scalar_tensor_tensor(bias3[:], bias_part[:, 2], kst[0:3, K_PART + 2:K_PART + 3], bias_some[:, 1],
                                     ALU.mult, ALU.add).then_inc(s_const, 1)
            dve.tensor_copy(tri[:], kst[:, K_TRI:K_TRI + P]).then_inc(s_const, 1)
            dve.tensor_copy(ones[:], kst[:, K_ONES:K_ONES + P]).then_inc(s_const, 1)
            dve.wait_ge(s_init, 7)
            dve.tensor_copy(place[:], place_i[:]).then_inc(s_const, 1)
            dve.wait_ge(s_const, 4)

            def products(g, rg):
                dve.wait_ge(s_qmm, done(g))
                dve.wait_ge(s_kv, done(g))
                k0 = kv[:, G * rg:G * rg + G, 0]
                window = bass.AP(k0.tensor, k0.offset, [list(k0.ap[0]), [2 * D, G], [2 * D, W], [1, D]])
                dve.tensor_tensor(prod[:], ps_q[:].unsqueeze(2).to_broadcast([P, G, W, D]), window,
                                  ALU.mult).then_inc(s_prod, 1)

            def scores(g):
                dve.wait_ge(s_prod, done(g))
                dve.tensor_reduce(sc[:], prod[:].rearrange("p g w (h d) -> p (g w h) d", h=HEADS),
                                  AX.X, ALU.add).then_inc(s_sc, 1)
                if isinstance(g, int) and g in (0, NG - 1):
                    dve.wait_ge(s_sc, done(g))
                    i, m = (2, mask_l) if g == 0 else (3, mask_r)
                    dve.tensor_scalar(sc[:, i], sc[:, i], m, None, ALU.mult).then_inc(s_msk, 1)
                    dve.wait_ge(s_msk, 1 if g == 0 else 2)

            def highest(g):
                if not isinstance(g, int) or 0 < g < NG - 1:
                    dve.wait_ge(s_sc, done(g))
                dve.tensor_reduce(smax[:], sc[:].rearrange("p g w h -> p g h w"), AX.X, ALU.max).then_inc(s_max, 1)

            def excess(g):
                dve.wait_ge(s_max, done(g))
                dve.tensor_tensor(dif[:], sc[:], smax[:].unsqueeze(2).to_broadcast([P, G, W, HEADS]),
                                  ALU.subtract).then_inc(s_dif, 1)

            def gate_best(h):
                apart(dve, done(h, 1))
                dve.wait_ge(s_logit, done(h, 1))
                for i in range(G):
                    ins = dve.max(top8[:, i], ps_s[:, 0, i])
                ins.then_inc(s_top, 1)

            def gate_which(h):
                apart(dve, done(h, 1))
                dve.wait_ge(s_top, done(h, 1))
                for i in range(G):
                    ins = dve.max_index(top8i[:, i], top8[:, i], ps_s[:, 0, i])
                ins.then_inc(s_topi, 1)
                wait(dve, s_gex, done(h - 1, 1))
                dve.tensor_tensor(gdif[:], top8[:], top8[:, :, 0:1].to_broadcast([P, G, E]), ALU.subtract).then_inc(s_gdif, 1)

            def gate_hot(h):
                dve.wait_ge(s_topi, done(h, 1))
                dve.tensor_tensor(hot[:], iota_e.unsqueeze(1).unsqueeze(1).to_broadcast([P, G, TOPK, E]),
                                  top8i[:, :, 0:TOPK].unsqueeze(3).to_broadcast([P, G, TOPK, E]),
                                  ALU.is_equal).then_inc(s_hot, 1)

            def gate_chosen(h):
                dve.wait_ge(s_hot, done(h, 1))
                wait(dve, s_pos, done(h - 1, 1))
                dve.tensor_tensor(chosen[:], hot[:, :, 0], hot[:, :, 1], ALU.add).then_inc(s_chosen, 1)

            def gate_count(h):
                dve.wait_ge(s_chosen, done(h, 1))
                dve.tensor_reduce(csum[:], chosen[:].rearrange("p g e -> p e g"), AX.X, ALU.add).then_inc(s_csum, 1)

            def gate_carry(h, rh):
                dve.wait_ge(s_csum, done(h, 1))
                dve.tensor_tensor(carry[:, rh % 2], carry[:, 1 - rh % 2], csum[:], ALU.add).then_inc(s_carry, 1)

            def gate_sum(h):
                dve.wait_ge(s_gex, done(h, 1))
                dve.tensor_reduce(gsum[:], gex[:], AX.X, ALU.add).then_inc(s_gsum, 1)

            def gate_labels(h, rh):
                dve.tensor_copy(x1g[:, rh, :, WHERE], place[:, bass.ds(h * G - G, G)])
                dve.tensor_copy(x1g[:, rh, :, FIRST], top8i[:, :, 0])

            def gate_recip(h):
                dve.wait_ge(s_gsum, done(h, 1))
                dve.reciprocal(grec[:], gsum[:]).then_inc(s_grec, 1)

            def gate_scores(h, rh):
                dve.wait_ge(s_grec, done(h, 1))
                dve.tensor_tensor(x1g[:, rh, :, SCORE:SCORE + TOPK], gex[:, :, 0:TOPK],
                                  grec[:].unsqueeze(2).to_broadcast([P, G, TOPK]), ALU.mult).then_inc(s_meta, 1)

            def gate_places(h):
                dve.wait_ge(s_pos, done(h, 1))
                dve.tensor_tensor(qpos[:], ps_s[:, 1], ebase.unsqueeze(1).to_broadcast([P, G, E]), ALU.add).then_inc(s_qpos, 1)

            def gate_hot_places(h):
                dve.wait_ge(s_qpos, done(h, 1))
                dve.tensor_tensor(hpos[:], hot[:], qpos[:].unsqueeze(2).to_broadcast([P, G, TOPK, E]), ALU.mult).then_inc(s_hpos, 1)

            def gate_slots(h, rh):
                dve.wait_ge(s_hpos, done(h, 1))
                wait(dve, s_queue[(rh - 2) % RING], slot_count(h - 2, (rh - 2) % RING, 16 * TOPK * G))
                with nc.allow_low_precision(reason="a whole number below 2 ** 24 among zeros"):
                    dve.tensor_reduce(slot[:, rh % 2], hpos[:], AX.X, ALU.add).then_inc(s_slot, 1)

            def soft_sum(g):
                dve.wait_ge(s_exp, done(g))
                dve.tensor_reduce(den[:], ex[:].rearrange("p g w h -> p g h w"), AX.X, ALU.add).then_inc(s_den, 1)

            def soft_recip(g):
                dve.wait_ge(s_den, done(g))
                dve.reciprocal(rden[:], den[:]).then_inc(s_rden, 1)

            def soft_prob(g):
                dve.wait_ge(s_rden, done(g))
                wait(dve, s_pv0, done(g - 1))
                dve.tensor_tensor(prob[:], ex[:], rden[:].unsqueeze(2).to_broadcast([P, G, W, HEADS]),
                                  ALU.mult).then_inc(s_prob, 1)

            def weigh(g, rg):
                dve.wait_ge(s_prob, done(g))
                wait(dve, s_atmm, done(g - 1))
                dve.tensor_tensor(pv[:, 2].rearrange("p g (h d) -> p g h d", h=HEADS),
                                  kv[:, G * rg + 2:G * rg + 2 + G, 1].rearrange("p g (h d) -> p g h d", h=HEADS),
                                  prob[:, :, 2].unsqueeze(3).to_broadcast([P, G, HEADS, HS]), ALU.mult).then_inc(s_pv, 1)

            def spread(kind, src):
                for i in range(G):
                    ins = dve.bn_stats(ln_st[:, kind, i], src[:, i])
                return ins

            def norms(t, r):
                gate = runs(t - 8, 1)
                if gate:
                    gate_places(t - 8)
                if isinstance(t, int) and t >= HUB:
                    gate_hot_places(t - 8)
                    gate_slots(t - 8, (r - 8) % RING)
                    return
                r2 = r % 2
                parts = []
                if runs(t):
                    apart(dve, in_count(t, r))
                    dve.wait_ge(s_xin[r], in_count(t, r))
                    if isinstance(t, int) and t == 0:
                        dve.wait_ge(s_edge, 32)
                    parts.append(0)
                    ins = spread(0, xin[:, r])
                if gate:
                    gate_hot_places(t - 8)
                if runs(t - 6, 1):
                    parts.append(2)
                if gate:
                    gate_slots(t - 8, (r - 8) % RING)
                if runs(t - 4, 1):
                    apart(dve, done(t - 4, 1))
                    dve.wait_ge(s_y, done(t - 4, 1))
                    parts.append(1)
                    ins = spread(1, ps_y)
                if parts != [2]:
                    ins.then_inc(s_bn, 1)
                if 2 in parts:
                    apart(dve, done(t - 6, 1))
                    dve.wait_ge(s_obn, done(t - 6, 1))
                upto_y = min(t, NG - 1 + 4) + 1 if isinstance(t, int) else t + 1
                apart(dve, upto_y)
                dve.wait_ge(s_bn, upto_y)
                for kind in parts:
                    for i in range(G):
                        ins = dve.bn_aggr(ln_mv[:, r2, kind, i], ln_st[:, kind, i])
                ins.then_inc(s_agg, 1)
                dve.wait_ge(s_agg, hub(t))
                wait(dve, s_rs, hub(t - 2) if not isinstance(t, int) or t >= 2 else 0)
                dve.tensor_tensor(ln_ve[:, r2], ln_mv[:, r2, :, :, 1], eps3.rearrange("p (k g) -> p k g", k=3),
                                  ALU.add).then_inc(s_ve, 1)

            def body(t, r):
                norms(t, r)
                g, rg, h, rh = t - 2, (r - 2) % RING, t - 7, (r - 7) % RING
                soft, gate = runs(g), runs(h, 1)
                if soft:
                    products(g, rg)
                if not isinstance(t, int) or t < HUB:
                    dve.wait_ge(s_rs, hub(t))
                    wait(dve, s_xh, done(t - 2))
                    wait(dve, s_yh, done(t - 6, 1))
                    wait(dve, s_x1, done(t - 8, 1))
                    dve.scalar_tensor_tensor(ln_nb[:, r % 2], ln_mv[:, r % 2, :, :, 0], -1.0, ln_rs[:, r % 2],
                                             ALU.mult, ALU.mult).then_inc(s_nb, 1)
                if soft:
                    scores(g)
                    highest(g)
                    excess(g)
                if gate:
                    gate_best(h)
                    gate_which(h)
                    gate_hot(h)
                    gate_labels(h, rh)
                    gate_chosen(h)
                if runs(t - 5, 1):
                    apart(dve, done(t - 5, 1))
                    dve.wait_ge(s_r3, done(t - 5, 1))
                    spread(2, r3[:, (r - 5) % 2]).then_inc(s_obn, 1)
                if soft:
                    soft_sum(g)
                if gate:
                    gate_count(h)
                if soft:
                    soft_recip(g)
                if gate:
                    gate_carry(h, rh)
                    gate_sum(h)
                if soft:
                    soft_prob(g)
                if gate:
                    gate_recip(h)
                    gate_scores(h, rh)
                if soft:
                    weigh(g, rg)

            pipeline(dve, body, NG + 8)

            dve.wait_ge(s_count, 1)
            dve.tensor_copy(n_e[:], ps_s_bank[:, 0, 0:E]).then_inc(s_tab, 1)
            tab = [1]

            def table(instruction, *args, **kw):
                dve.wait_ge(s_tab, tab[0])
                instruction(*args, **kw).then_inc(s_tab, 1)
                tab[0] += 1

            def row(first, n):
                return kst[:, first:first + n]

            def each_e(ap):
                return ap.unsqueeze(1).to_broadcast([P, BLOCKS, E])

            def each_b(ap):
                return ap.unsqueeze(2).to_broadcast([P, BLOCKS, E])

            with nc.allow_low_precision(reason="whole numbers below 2 ** 24"):
                table(dve.tensor_tensor, pad_at[:], n_e[:], row(K_EBASE, E), ALU.add)
                table(dve.tensor_scalar, nblk_u[:, 0], n_e[:], float(BS - 1), None, ALU.add)
                table(dve.tensor_scalar, nblk_u[:, 1], nblk_u[:, 0], BS.bit_length() - 1, None, ALU.logical_shift_right)
                table(dve.tensor_copy, nblk[:], nblk_u[:, 1])
                table(dve.tensor_tensor, before[:], row(K_BEFORE, E * E).rearrange("o (e j) -> o e j", e=E),
                      nblk[:].unsqueeze(1).to_broadcast([P, E, E]), ALU.mult)
                table(dve.tensor_reduce, start[:], before[:], AX.X, ALU.add)
                table(dve.tensor_tensor, end[:], start[:], nblk[:], ALU.add)
                table(dve.scalar_tensor_tensor, offs[:], start[:], -float(BS), row(K_EBASE, E), ALU.mult, ALU.add)
                table(dve.tensor_tensor, b_ge[:], each_b(row(K_BLOCK, BLOCKS)), each_e(start[:]), ALU.is_ge)
                table(dve.tensor_tensor, b_lt[:], each_b(row(K_BLOCK, BLOCKS)), each_e(end[:]), ALU.is_lt)
                table(dve.tensor_tensor, b_in[:], b_ge[:], b_lt[:], ALU.mult)
                table(dve.tensor_tensor, b_v[:, 1], b_in[:], each_e(row(K_IOTA, E)), ALU.mult)
                table(dve.tensor_tensor, b_v[:, 0], each_b(row(K_START, BLOCKS)), each_e(offs[:]), ALU.add)
                table(dve.tensor_tensor, b_v[:, 0], b_v[:, 0], b_in[:], ALU.mult)
                table(dve.tensor_reduce, b_sum[:], b_v[:], AX.X, ALU.add)
                table(dve.tensor_copy, b_expert[:], b_sum[:, 1])
                table(dve.tensor_scalar, b_row[:], b_sum[:, 0], float(NULL), None, ALU.add)
            assert tab[0] == TABLE

            def weights_of(b, rb):
                q = rb % RING
                dve.wait_ge(s_xs[rb], ring_count(b, rb, RING3, 16))
                wait(dve, s_xsc, upto(b - RING))
                expert = b_sum[:, 1, bass.ds(b, 1)]
                first = xs[:, rb, :, FIRST]
                dve.scalar_tensor_tensor(part[:, q, 0], first, expert, xs[:, rb, :, SCORE], ALU.is_equal, ALU.mult)
                dve.scalar_tensor_tensor(part[:, q, 1], first, expert, xs[:, rb, :, SCORE + 1], ALU.not_equal,
                                         ALU.mult).then_inc(s_part, 1)
                dve.wait_ge(s_part, upto(b))
                dve.tensor_tensor(xscore[:, q], part[:, q, 0], part[:, q, 1], ALU.add).then_inc(s_xscore, 1)
                wait(dve, s_back[rb], ring_count(b - RING3, rb, RING3, 32))
                dve.scalar_tensor_tensor(where[:, rb], first, expert, xs[:, rb, :, WHERE], ALU.not_equal,
                                         ALU.add).then_inc(s_where, 1)

            def body(t, r):
                q = r % 2
                if has(t + 2):
                    weights_of(t + 2, (r + 2) % RING3)
                b = t
                if has(b):
                    dve.wait_ge(s_xst, upto(b))
                    wait(dve, s_hmm, upto(b - 2))
                    n = 3 if has(b, C) else 2
                    dve.tensor_copy(xsT[:, q, 0:n], ps_x[q][:, 0:n]).then_inc(s_xsT, 1)
                b, rb = t - 1, (r - 1) % RING3
                if has(b):
                    dve.wait_ge(s_silu, upto(b))
                    wait(dve, s_omm, upto(b - RING))
                    n = 3 if has(b, C) else 2
                    dve.tensor_tensor(hid[:, rb % RING, 0:n], silu[:, rb % 2, 0:n], ps_h3[rb % 2][:, 0:n], ALU.mult).then_inc(s_hid, 1)
                b, rb = t - 2, (r - 2) % RING3
                if has(b, C):
                    dve.wait_ge(s_ys, upto(b))
                    col = tokens(b)
                    dve.tensor_tensor(col, col, ps_o[rb % 2][:, 2], ALU.add).then_inc(s_sh, 1)

            weights_of(0, 0)
            weights_of(1, 1)
            over_blocks(dve, body, BLOCKS + 2)
            dve.wait_ge(s_sh, C)

            def body(t, r):
                if has(t, NG4):
                    at = t * G
                    o = x1[:, bass.ds(at, G)]
                    dve.wait_ge(s_ysum, upto(t, NG4))
                    dve.tensor_tensor(o, o, ysum[:, r % 2], ALU.add).then_inc(s_o, 1)
                g, rg = t - 1, (r - 1) % RING
                if has(g, NG4):
                    apart(dve, upto(g, NG4))
                    dve.wait_ge(s_o, upto(g, NG4))
                    wait(dve, s_lmv, upto(g - 1, NG4))
                    for i in range(G):
                        ins = dve.bn_stats(l_st[:, i], tokens(g * G + i))
                    ins.then_inc(s_lst, 1)
                g, rg = t - 2, (r - 2) % RING
                if has(g, NG4):
                    wait(dve, s_lnb, upto(t - 1 - RING, NG4))
                    dve.wait_ge(s_lmv, upto(g, NG4))
                    dve.tensor_tensor(l_ve[:, rg], l_mv[:, rg, :, 1], eps3[:, 2 * G:3 * G], ALU.add).then_inc(s_lve, 1)
                g, rg = t - 4, r
                if has(g, NG4):
                    dve.wait_ge(s_lrs, upto(g, NG4))
                    wait(dve, s_on, upto(g - RING, NG4))
                    dve.scalar_tensor_tensor(l_nb[:, rg], l_mv[:, rg, :, 0], -1.0, l_rs[:, rg], ALU.mult, ALU.mult).then_inc(s_lnb, 1)
                g, rg = t - 1, (r - 1) % RING
                if has(g, NG4):
                    apart(dve, upto(g, NG4))
                    dve.wait_ge(s_lst, upto(g, NG4))
                    for i in range(G):
                        ins = dve.bn_aggr(l_mv[:, rg, i], l_st[:, i])
                    ins.then_inc(s_lmv, 1)

            over_output(dve, body, NG4 + 4)

        @block.scalar
        def _(act):
            act.wait_ge(s_w, 16)
            act.wait_ge(s_init, 7)
            act.preload_act_table_set(EXP_LN)

            def inverse_roots(t, r):
                act.wait_ge(s_ve, hub(t))
                act.activation(ln_log[:], ln_ve[:, r % 2], ACT.Ln).then_inc(s_log, 1)
                act.wait_ge(s_log, hub(t))
                wait(act, s_nb, hub(t - 2) if not isinstance(t, int) or t >= 2 else 0)
                act.activation(ln_rs[:, r % 2], ln_log[:], ACT.Exp, scale=-0.5).then_inc(s_rs, 1)

            def body(t, r):
                l2 = (r - 1) % 2
                g = t - 3
                if runs(g):
                    act.wait_ge(s_dif, done(g))
                    wait(act, s_prob, done(g - 1))
                    act.activation(ex[:], dif[:], ACT.Exp, scale=float(1.0 / np.sqrt(HS))).then_inc(s_exp, 1)
                g = t - 8
                if runs(g, 1):
                    act.wait_ge(s_gdif, done(g, 1))
                    wait(act, s_meta, done(g - 1, 1))
                    act.activation(gex[:], gdif[:], ACT.Exp).then_inc(s_gex, 1)
                g, rg = t - 1, (r - 1) % RING
                if runs(g):
                    act.wait_ge(s_nb, hub(t - 1))
                    wait(act, s_xt, done(g - 2))
                    for i in range(G):
                        ins = act.activation(xh[:, rg % 2, i], xin[:, rg, i], ACT.Identity,
                                             bias=ln_nb[:, l2, 0, i:i + 1], scale=ln_rs[:, l2, 0, i:i + 1])
                    ins.then_inc(s_xh, 1)
                g, rg = t - 7, (r - 7) % RING
                if runs(g, 1):
                    act.wait_ge(s_nb, hub(t - 1))
                    wait(act, s_x1st[rg], slot_count(g - RING, rg))
                    wait(act, s_queue[rg], slot_count(g - RING, rg, 16 * TOPK * G))
                    for i in range(G):
                        ins = act.activation(x1g[:, rg, i, 0:D], r3[:, rg % 2, i], ACT.Identity,
                                             bias=ln_nb[:, l2, 2, i:i + 1], scale=ln_rs[:, l2, 2, i:i + 1])
                    ins.then_inc(s_x1, 1)
                if isinstance(t, int) and t < RING:
                    inverse_roots(t, r)
                g, rg = t - 5, (r - 5) % RING
                if runs(g, 1):
                    act.wait_ge(s_yt, done(g, 1))
                    wait(act, s_z, done(g - 2, 1))
                    act.activation(yT[:, rg % 2], ps_z[:], ACT.Identity, bias=lnp[:, 3:4], scale=lnp[:, 2:3]).then_inc(s_yT, 1)
                g, rg = t - 1, (r - 1) % RING
                if runs(g):
                    act.wait_ge(s_xt, done(g))
                    wait(act, s_y, done(g - 3, 1))
                    act.activation(xT[:, rg], ps_t0[:], ACT.Identity, bias=lnp[:, 1:2], scale=lnp[:, 0:1]).then_inc(s_xT, 1)
                g, rg = t - 5, (r - 5) % RING
                if runs(g, 1):
                    act.wait_ge(s_z, done(g, 1))
                    wait(act, s_r3, done(g - 2, 1))
                    act.activation(gz[:, rg % 2], ps_z[:], ACT.Gelu).then_inc(s_gz, 1)
                    act.preload_act_table_set(EXP_LN)
                g, rg = t - 7, (r - 7) % RING
                if runs(g, 1):
                    act.wait_ge(s_x1t, done(g, 1))
                    wait(act, s_logit, done(g - 2, 1))
                    act.activation(x1T[:, rg % 2], ps_t0[:], ACT.Identity).then_inc(s_x1T, 1)
                if not isinstance(t, int) or RING <= t < HUB:
                    inverse_roots(t, r)
                g, rg = t - 3, (r - 3) % RING
                if runs(g):
                    act.wait_ge(s_atmm, done(g))
                    wait(act, s_y, done(g - 1, 1))
                    act.activation(at[:, rg % 2], ps_t1[:], ACT.Identity).then_inc(s_at, 1)
                g, rg = t - 4, (r - 4) % RING
                if runs(g, 1):
                    act.wait_ge(s_nb, hub(t))
                    wait(act, s_yt, done(g - 2, 1))
                    for i in range(G):
                        ins = act.activation(yh[:, rg % 2, i], ps_y[:, i], ACT.Identity,
                                             bias=ln_nb[:, r % 2, 1, i:i + 1], scale=ln_rs[:, r % 2, 1, i:i + 1])
                    ins.then_inc(s_yh, 1)
                g, rg = t - 1, (r - 1) % RING
                if runs(g):
                    act.wait_ge(s_kvmm, done(g))
                    wait(act, s_pv, done(g - 3))
                    wait(act, s_pv0, done(g - 3))
                    at0 = 2 + G * rg
                    if isinstance(g, int) and g == 0:
                        act.activation(kv[:, at0:at0 + 2], ps_kv[:, 0:2], ACT.Identity, scale=mask_l)
                        act.activation(kv[:, at0 + 2:at0 + 4], ps_kv[:, 2:4], ACT.Identity).then_inc(s_kv, 1)
                    elif isinstance(g, int) and g == NG - 1:
                        act.activation(kv[:, at0:at0 + 2], ps_kv[:, 0:2], ACT.Identity)
                        act.activation(kv[:, at0 + 2:at0 + 4], ps_kv[:, 2:4], ACT.Identity, scale=mask_r).then_inc(s_kv, 1)
                    else:
                        ins = act.activation(kv[:, at0:at0 + G], ps_kv[:], ACT.Identity)
                        if rg == RING - 1:
                            ins = act.activation(kv[:, 0:2], ps_kv[:, 2:4], ACT.Identity)
                        ins.then_inc(s_kv, 1)

            pipeline(act, body, NG + 8)
            act.wait_ge(s_wx, 16)
            act.wait_ge(s_tab, TABLE)

            def scale(b, rb):
                if has(b):
                    act.wait_ge(s_xscore, upto(b))
                    wait(act, s_xst, upto(b - 2))
                    for u in range(2):
                        ins = act.activation(xsc[:, rb % 2, u], xs[:, rb, u, 0:D], ACT.Identity, scale=xscore[:, rb % RING, u:u + 1])
                    ins.then_inc(s_xsc, 1)

            def body(t, r):
                scale(t + 1, (r + 1) % RING3)
                b, rb = t, r
                if has(b):
                    wait(act, s_omm, upto(b - RING))
                    e = act.value_load(b_expert[0:1, bass.ds(b, 1)], min_val=0, max_val=E - 1)
                    act.activation(wst[:, rb % RING], wall[:, :, bass.ds(e, 1)].rearrange("p w o d -> p w (o d)"),
                                   ACT.Identity).then_inc(s_wst, 1)
                b, rb = t - 1, (r - 1) % RING3
                if has(b):
                    act.wait_ge(s_hmm, upto(b))
                    wait(act, s_hid, upto(b - 2))
                    n = 3 if has(b, C) else 2
                    act.activation(silu[:, rb % 2, 0:n], ps_h1[rb % 2][:, 0:n],
                                   ACT.Silu).then_inc(s_silu, 1)
                b, rb = t - 2, (r - 2) % RING3
                if has(b):
                    act.wait_ge(s_omm, upto(b))
                    wait(act, s_back[(rb - RING) % RING3], ring_count(b - RING, (rb - RING) % RING3, RING3, 32))
                    act.activation(ys[:, rb % RING], ps_o[rb % 2][:, 0:2], ACT.Identity).then_inc(s_ys, 1)

            scale(0, 0)
            over_blocks(act, body, BLOCKS + 2)

            def body(t, r):
                g, rg = t - 4, r
                if has(g, NG4):
                    act.wait_ge(s_lnb, upto(g, NG4))
                    wait(act, s_out[rg], ring_count(g - RING, rg, RING, 16))
                    for i in range(G):
                        ins = act.activation(on[:, rg, i], tokens(g * G + i), ACT.Identity,
                                             bias=l_nb[:, rg, i:i + 1], scale=l_rs[:, rg, i:i + 1])
                    ins.then_inc(s_on, 1)

            over_output(act, body, NG4 + 4)

        @block.tensor
        def _(pe):
            ones3 = ones[0:3, :]

            def bias(out, part, width, copies):
                row = bias3[:, part * D:part * D + width].unsqueeze(1).to_broadcast([3, copies, width])
                pe.matmul(out, ones3, row, start=True, stop=False, skip_group_check=True)

            def add(out, lhsT, rhs, stop):
                return pe.matmul(out, lhsT, rhs, start=False, stop=stop, skip_group_check=True)

            def keep_warm(products):
                for _ in range(products):
                    pe.matmul(ps_s_bank[:], ones[:], ones[:].unsqueeze(1).to_broadcast([P, G, P]), start=True, stop=True)

            pe.wait_ge(s_w, 16)
            pe.wait_ge(s_const, 3)
            pe.wait_ge(s_init, 7)
            keep_warm(9)

            def body(t, r):
                g, rg = t - 4, (r - 4) % RING
                if runs(g, 1):
                    pe.wait_ge(s_at, done(g))
                    wait(pe, s_yh, done(g - 1, 1))
                    rp = (rg - 1) % RING
                    bias(ps_y[:], 3, D, G)
                    for i in range(G):
                        add(ps_y[:, i], xT[:, rp, i + 2] if i < 2 else xT[:, rg, i - 2], ident, False)
                        add(ps_y[:, i], at[:, rp % 2, i + 2] if i < 2 else at[:, rg % 2, i - 2], wfb[:, 0], False)
                        mm = add(ps_y[:, i], at[:, rg % 2, i], wfb[:, 1], True)
                    mm.then_inc(s_y, 1)
                g, rg = t - 5, (r - 5) % RING
                if runs(g, 1):
                    pe.wait_ge(s_yh, done(g, 1))
                    wait(pe, s_gz, done(g - 1, 1))
                    for i in range(G):
                        mm = pe.transpose(ps_z[:, i], yh[:, rg % 2, i], ident)
                    mm.then_inc(s_yt, 1)
                g, rg = t - 8, (r - 8) % RING
                if runs(g, 1):
                    pe.wait_ge(s_chosen, done(g, 1))
                    wait(pe, s_carry, done(g - 1, 1))
                    pe.matmul(ps_s[:, 1], tri[:], chosen[:], start=True, stop=False, skip_group_check=True)
                    for i in range(G - 1):
                        add(ps_s[:, 1, i + 1:G], ones[:], chosen[:, i:i + 1].to_broadcast([P, G - 1 - i, E]), False)
                    add(ps_s[:, 1], ones[:], carry[:, 1 - rg % 2].unsqueeze(1).to_broadcast([P, G, E]), True).then_inc(s_pos, 1)
                g, rg = t - 1, (r - 1) % RING
                if runs(g):
                    pe.wait_ge(s_xh, done(g))
                    wait(pe, s_x1T, done(t - 8, 1))
                    for i in range(G):
                        mm = pe.transpose(ps_t0[:, i], xh[:, rg % 2, i], ident)
                    mm.then_inc(s_xt, 1)
                if isinstance(t, int) and 1 <= t < 5:
                    keep_warm(3)
                g, rg = t - 5, (r - 5) % RING
                if runs(g, 1):
                    pe.wait_ge(s_yT, done(g, 1))
                    bias(ps_z[:], 4, D, G)
                    for i in range(G):
                        mm = add(ps_z[:, i], yT[:, rg % 2, i], wo, True)
                    mm.then_inc(s_z, 1)
                g, rg = t - 7, (r - 7) % RING
                if runs(g, 1):
                    pe.wait_ge(s_x1, done(g, 1))
                    wait(pe, s_xT, done(t - 1))
                    for i in range(G):
                        mm = pe.transpose(ps_t0[:, i], x1g[:, rg, i, 0:D], ident)
                    mm.then_inc(s_x1t, 1)
                g, rg = t - 3, (r - 3) % RING
                if runs(g):
                    pe.wait_ge(s_pv, done(g))
                    pe.wait_ge(s_pv0, done(g))
                    wait(pe, s_at, done(g - 1))
                    for i in range(G):
                        for j in range(W):
                            mm = pe.matmul(ps_t1[:, i], pv[:, j, i], ident, start=(j == 0), stop=(j == W - 1))
                    mm.then_inc(s_atmm, 1)
                g, rg = t - 1, (r - 1) % RING
                if runs(g):
                    pe.wait_ge(s_xT, done(g))
                    wait(pe, s_kv, done(g - 1))
                    for h in range(2):
                        bias(ps_kv[:, 2 * h:2 * h + 2].rearrange("p g k d -> p g (k d)"), 1, 2 * D, 2)
                        for i in range(2 * h, 2 * h + 2):
                            mm = add(ps_kv[:, i].rearrange("p k d -> p (k d)"), xT[:, rg, i], wqkv[:, D:3 * D], True)
                    mm.then_inc(s_kvmm, 1)
                g, rg = t - 7, (r - 7) % RING
                if runs(g, 1):
                    pe.wait_ge(s_x1T, done(g, 1))
                    wait(pe, s_qpos, done(g - 1, 1))
                    for i in range(G):
                        mm = pe.matmul(ps_s[:, 0, i], x1T[:, rg % 2, i], gate_t, start=True, stop=True, skip_group_check=True)
                    mm.then_inc(s_logit, 1)
                g, rg = t - 1, (r - 1) % RING
                if runs(g):
                    wait(pe, s_prod, done(g - 1))
                    bias(ps_q[:], 0, D, G)
                    for i in range(G):
                        mm = add(ps_q[:, i], xT[:, (rg - 1) % RING, G - 1] if i == 0 else xT[:, rg, i - 1], wqkv[:, 0:D], True)
                    mm.then_inc(s_qmm, 1)
                if isinstance(t, int) and 1 <= t < 5:
                    keep_warm(6)

            pipeline(pe, body, NG + 8)

            pe.wait_ge(s_carry, NG - 1)
            pe.wait_ge(s_hpos, NG - 1)
            pe.matmul(ps_s_bank[:, 0, 0:E], ones[:], carry[:, (NG - 1) % 2], start=True, stop=True).then_inc(s_count, 1)
            pe.wait_ge(s_wx, 16)
            pe.wait_ge(s_tab, 1)
            pe.wait_ge(s_tab, TABLE)
            keep_warm(44)

            def body(t, r):
                b, rb = t, r
                if has(b):
                    pe.wait_ge(s_xsc, upto(b))
                    wait(pe, s_xsT, upto(b - 2))
                    for u in range(2):
                        mm = pe.transpose(ps_x[rb % 2][:, u], xsc[:, rb % 2, u], ident)
                    if has(b, C):
                        pe.wait_ge(s_xc[rb], ring_count(b, rb, RING3, 16))
                        mm = pe.transpose(ps_x[rb % 2][:, 2], xc[:, rb], ident)
                    mm.then_inc(s_xst, 1)
                b, rb = t - 1, (r - 1) % RING3
                if has(b):
                    q = rb % 2
                    pe.wait_ge(s_xsT, upto(b))
                    pe.wait_ge(s_wst, upto(b))
                    wait(pe, s_hid, upto(b - 2))
                    h1 = ps_h1[q]
                    for w, ps in ((0, h1), (1, ps_h3[q])):
                        mm = pe.matmul(ps[:, 0:2], wst[:, rb % RING, w], xsT[:, q, 0:2], start=True, stop=True)
                        if has(b, C):
                            mm = pe.matmul(ps[:, 2], wsh[:, w], xsT[:, q, 2], start=True, stop=True)
                    mm.then_inc(s_hmm, 1)
                b, rb = t - 2, (r - 2) % RING3
                if has(b):
                    pe.wait_ge(s_hid, upto(b))
                    wait(pe, s_ys, upto(b - 2))
                    wait(pe, s_sh, upto(b - 2, C))
                    for u in range(2):
                        mm = pe.matmul(ps_o[rb % 2][:, u], hid[:, rb % RING, u], wst[:, rb % RING, 2], start=True, stop=True)
                    if has(b, C):
                        mm = pe.matmul(ps_o[rb % 2][:, 2], hid[:, rb % RING, 2], wsh[:, 2], start=True, stop=True)
                    mm.then_inc(s_omm, 1)

            over_blocks(pe, body, BLOCKS + 2)


def kernel(**inputs):
    import concourse.bacc as _bacc
    from concourse.bass_utils import run_bass_kernel_spmd as _run

    nc = _bacc.Bacc("TRN2", target_bir_lowering=False, num_devices=1)
    arrays, a = {}, {}
    x = "L0_attn_input_feature"
    for name, value in {x: inputs[x], **pack(inputs)}.items():
        value = np.ascontiguousarray(value)
        arrays[f"in_{name}"] = value
        a[name] = nc.dram_tensor(f"in_{name}", value.shape, mybir.dt.from_np(value.dtype), kind="ExternalInput").ap()
    a["queue_dram"] = nc.dram_tensor("queue_dram", (NULL + BS, ROW), F32).ap()
    a["back_dram"] = nc.dram_tensor("back_dram", (NB * T * TOPK, D), F32).ap()
    a["out"] = nc.dram_tensor("out_0", (NB, T, D), F32, kind="ExternalOutput").ap()
    build(nc, a)
    return _run(nc, [arrays], core_ids=[0]).results[0]["out_0"]
```
